# Optimizing a Trainium2 kernel written in Bass

```python
import numpy as np
import jax
import jax.numpy as jnp

def _softmax(x, axis=-1):
    return jax.nn.softmax(x, axis=axis)

def _gelu(x):
    return jax.nn.gelu(x, approximate=True)

def _silu(x):
    return jax.nn.silu(x)

def _sigmoid(x):
    return jax.nn.sigmoid(x)

def _layernorm(x, axis=-1, eps=1e-05):
    m = jnp.mean(x, axis=axis, keepdims=True)
    v = jnp.var(x, axis=axis, keepdims=True)
    return (x - m) / jnp.sqrt(v + eps)

def _scatter_add(tgt, idx, src, axis=0):
    return tgt.at[idx].add(src)

def _segment_sum(src, seg, n):
    return jax.ops.segment_sum(src, seg, n)
kernel_name = 'mk_xattn_seq_d2_seqx_r8_b47711'

def setup_inputs(seed: int=0):
    np.random.seed(seed)
    _w = jnp.asarray

    def _rec_inputs():
        import jax
        import jax.numpy as jnp
        _rk = jax.random.key(seed)
        x = -0.0002928 + 1 * jax.random.normal(jax.random.fold_in(_rk, 1), (128, 64, 128), jnp.float32)
        _lenS = 64 - jax.random.randint(jax.random.fold_in(_rk, 7), (128,), 0, max(1, 64 // 4) + 1, jnp.int32)
        _lenS2 = 64 - jax.random.randint(jax.random.fold_in(_rk, 8), (128,), 0, max(1, 64 // 4) + 1, jnp.int32)
        _ctx_1024P = jax.random.normal(jax.random.fold_in(_rk, 11), (128, 16, 128), jnp.float32)
        _ctx_1024c = jax.random.dirichlet(jax.random.fold_in(_rk, 511), 0.3 * jnp.ones((16,), jnp.float32), (128, 64))
        _ctx_1024t = jnp.einsum('bsk,bkd->bsd', _ctx_1024c, _ctx_1024P)
        _ctx_1024t = _ctx_1024t * jax.lax.rsqrt(jnp.mean(jnp.square(_ctx_1024t)) + 1e-12) * 0.953939
        ctx_1024 = -1.39393e-06 + 0.999914 * (_ctx_1024t + 0.3 * jax.random.normal(jax.random.fold_in(_rk, 611), (128, 64, 128), jnp.float32))
        _validS = jnp.arange(64)[None, :] < _lenS[:, None]
        _validS2 = jnp.arange(64)[None, :] < _lenS2[:, None]
        _causal = jnp.tril(jnp.ones((64, 64), dtype=bool))
        mask_Bx1xSxS2_bk0 = jnp.logical_not(jnp.broadcast_to(_validS2[:, None, None, :], (128, 1, 64, 64)))
        mask_Bx1xSxS2_bf1 = jnp.ones((128, 1, 64, 64), dtype=bool)
        return (x, ctx_1024, mask_Bx1xSxS2_bk0, mask_Bx1xSxS2_bf1)
    x, ctx_1024, mask_Bx1xSxS2_bk0, mask_Bx1xSxS2_bf1 = _rec_inputs()

    def _L0_xattn_setup():
        import jax, jax.numpy as jnp
        import numpy as np
        import math
        B, L, D, H, DFF = (2, 256, 128, 16, 512)

        def _mha(xq, xkv, Wq, bq, Wk, bk, Wv, bv, Wo, bo, mask, h):
            b, lq, d = xq.shape
            dk = d // h
            q = (xq @ Wq + bq).reshape(b, lq, h, dk).transpose(0, 2, 1, 3)
            k = (xkv @ Wk + bk).reshape(b, -1, h, dk).transpose(0, 2, 1, 3)
            v = (xkv @ Wv + bv).reshape(b, -1, h, dk).transpose(0, 2, 1, 3)
            scores = jnp.einsum('bhqd,bhkd->bhqk', q, k) / jnp.sqrt(jnp.float32(dk))
            scores = jnp.where(mask, scores, jnp.float32(-1000000000.0))
            prob = jax.nn.softmax(scores, axis=-1)
            out = jnp.einsum('bhqk,bhkd->bhqd', prob, v)
            out = out.transpose(0, 2, 1, 3).reshape(b, lq, d)
            return out @ Wo + bo
        key = jax.random.key(seed)
        ks = jax.random.split(key, 16)
        s = 0.02
        inp = {'tgt': jax.random.normal(ks[0], (B, L, D), jnp.float32), 'encoder_out': jax.random.normal(ks[1], (B, L, D), jnp.float32), 'tgt_mask': jnp.broadcast_to(jnp.tril(jnp.ones((L, L), bool)), (B, 1, L, L)), 'src_tgt_mask': jnp.ones((B, 1, L, L), bool)}
        names = ['sWq', 'sWk', 'sWv', 'sWo', 'cWq', 'cWk', 'cWv', 'cWo']
        for i, n in enumerate(names):
            inp[n] = s * jax.random.normal(ks[2 + i], (D, D), jnp.float32)
            inp['sb' + n[2] if n[0] == 's' else 'cb' + n[2]] = jnp.zeros((D,), jnp.float32)
        inp['W1'] = s * jax.random.normal(ks[10], (D, DFF), jnp.float32)
        inp['b1'] = jnp.zeros((DFF,), jnp.float32)
        inp['W2'] = s * jax.random.normal(ks[11], (DFF, D), jnp.float32)
        inp['b2'] = jnp.zeros((D,), jnp.float32)
        return inp
    _L0_xattn_all = _L0_xattn_setup()
    _L0_xattn_in = {k: v for k, v in _L0_xattn_all.items() if k in ('sWq', 'sbq', 'sWk', 'sbk', 'sWv', 'sbv', 'sWo', 'sbo', 'cWq', 'cbq', 'cWk', 'cbk', 'cWv', 'cbv', 'cWo', 'cbo', 'W1', 'b1', 'W2', 'b2')}
    del _L0_xattn_all

    def _L1_xattn_setup():
        import jax, jax.numpy as jnp
        import numpy as np
        NEG = -1e+32
        EPS_LN = 1e-05

        def _layer_norm(x, w, b):
            mu = jnp.mean(x, axis=-1, keepdims=True)
            var = jnp.mean((x - mu) ** 2, axis=-1, keepdims=True)
            return (x - mu) / jnp.sqrt(var + EPS_LN) * w + b

        def _forward(query, key, values, Wk, bk, Wv, bv, Wo, bo, gammas, ln1_w, ln1_b, W1, b1, W2, b2, ln2_w, ln2_b, mask):
            B, S, D = query.shape
            H = gammas.shape[0]
            dk = D // H

            def proj(x, W, b):
                return (x @ W.T + b).reshape(B, S, H, dk).transpose(0, 2, 1, 3)
            q = proj(query, Wk, bk)
            k = proj(key, Wk, bk)
            v = proj(values, Wv, bv)
            scores = jnp.einsum('bhqd,bhkd->bhqk', q, k) / np.sqrt(dk).astype(np.float32)
            allow = jnp.tril(jnp.ones((S, S), bool), k=mask - 1)[None, None]
            scores_ = jax.nn.softmax(jnp.where(allow, scores, NEG), axis=-1)
            scores_ = scores_ * allow.astype(scores_.dtype)
            distcum = jnp.cumsum(scores_, axis=-1)
            disttotal = jnp.sum(scores_, axis=-1, keepdims=True)
            idx = jnp.arange(S)
            position_effect = jnp.abs(idx[:, None] - idx[None, :]).astype(jnp.float32)[None, None]
            dist_scores = jnp.sqrt(jnp.clip((disttotal - distcum) * position_effect, 0.0, None))
            gamma = -jax.nn.softplus(gammas)[None]
            total_effect = jnp.clip(jnp.exp(dist_scores * gamma), 1e-05, 100000.0)
            total_effect = jax.lax.stop_gradient(total_effect)
            scores = scores * total_effect
            scores = jnp.where(allow, scores, NEG)
            attn = jax.nn.softmax(scores, axis=-1)
            out = jnp.einsum('bhqk,bhkd->bhqd', attn, v)
            concat = out.transpose(0, 2, 1, 3).reshape(B, S, D)
            query2 = concat @ Wo.T + bo
            x = _layer_norm(query + query2, ln1_w, ln1_b)
            ff = jax.nn.relu(x @ W1.T + b1) @ W2.T + b2
            x = _layer_norm(x + ff, ln2_w, ln2_b)
            return x
        key = jax.random.key(seed)
        ks = jax.random.split(key, 10)
        B, S, D, H, F = (2, 256, 128, 16, 512)
        s = 0.02
        return {'query': jax.random.normal(ks[0], (B, S, D), jnp.float32), 'key': jax.random.normal(ks[1], (B, S, D), jnp.float32), 'values': jax.random.normal(ks[2], (B, S, D), jnp.float32), 'Wk': jax.random.normal(ks[3], (D, D), jnp.float32) * s, 'bk': jnp.zeros((D,), jnp.float32), 'Wv': jax.random.normal(ks[4], (D, D), jnp.float32) * s, 'bv': jnp.zeros((D,), jnp.float32), 'Wo': jax.random.normal(ks[5], (D, D), jnp.float32) * s, 'bo': jnp.zeros((D,), jnp.float32), 'gammas': jax.random.normal(ks[6], (H, 1, 1), jnp.float32), 'ln1_w': jnp.ones((D,), jnp.float32), 'ln1_b': jnp.zeros((D,), jnp.float32), 'W1': jax.random.normal(ks[7], (F, D), jnp.float32) * s, 'b1': jnp.zeros((F,), jnp.float32), 'W2': jax.random.normal(ks[8], (D, F), jnp.float32) * s, 'b2': jnp.zeros((D,), jnp.float32), 'ln2_w': jnp.ones((D,), jnp.float32), 'ln2_b': jnp.zeros((D,), jnp.float32), 'mask': 1}
    _L1_xattn_all = _L1_xattn_setup()
    _L1_xattn_in = {k: v for k, v in _L1_xattn_all.items() if k in ('Wk', 'bk', 'Wv', 'bv', 'Wo', 'bo', 'gammas', 'ln1_w', 'ln1_b', 'W1', 'b1', 'W2', 'b2', 'ln2_w', 'ln2_b')}
    del _L1_xattn_all
    return {'x': x, 'ctx_1024': ctx_1024, 'mask_Bx1xSxS2_bk0': mask_Bx1xSxS2_bk0, 'mask_Bx1xSxS2_bf1': mask_Bx1xSxS2_bf1, 'L0_xattn_sWq': _L0_xattn_in['sWq'], 'L0_xattn_sbq': _L0_xattn_in['sbq'], 'L0_xattn_sWk': _L0_xattn_in['sWk'], 'L0_xattn_sbk': _L0_xattn_in['sbk'], 'L0_xattn_sWv': _L0_xattn_in['sWv'], 'L0_xattn_sbv': _L0_xattn_in['sbv'], 'L0_xattn_sWo': _L0_xattn_in['sWo'], 'L0_xattn_sbo': _L0_xattn_in['sbo'], 'L0_xattn_cWq': _L0_xattn_in['cWq'], 'L0_xattn_cbq': _L0_xattn_in['cbq'], 'L0_xattn_cWk': _L0_xattn_in['cWk'], 'L0_xattn_cbk': _L0_xattn_in['cbk'], 'L0_xattn_cWv': _L0_xattn_in['cWv'], 'L0_xattn_cbv': _L0_xattn_in['cbv'], 'L0_xattn_cWo': _L0_xattn_in['cWo'], 'L0_xattn_cbo': _L0_xattn_in['cbo'], 'L0_xattn_W1': _L0_xattn_in['W1'], 'L0_xattn_b1': _L0_xattn_in['b1'], 'L0_xattn_W2': _L0_xattn_in['W2'], 'L0_xattn_b2': _L0_xattn_in['b2'], 'L1_xattn_Wk': _L1_xattn_in['Wk'], 'L1_xattn_bk': _L1_xattn_in['bk'], 'L1_xattn_Wv': _L1_xattn_in['Wv'], 'L1_xattn_bv': _L1_xattn_in['bv'], 'L1_xattn_Wo': _L1_xattn_in['Wo'], 'L1_xattn_bo': _L1_xattn_in['bo'], 'L1_xattn_gammas': _L1_xattn_in['gammas'], 'L1_xattn_ln1_w': _L1_xattn_in['ln1_w'], 'L1_xattn_ln1_b': _L1_xattn_in['ln1_b'], 'L1_xattn_W1': _L1_xattn_in['W1'], 'L1_xattn_b1': _L1_xattn_in['b1'], 'L1_xattn_W2': _L1_xattn_in['W2'], 'L1_xattn_b2': _L1_xattn_in['b2'], 'L1_xattn_ln2_w': _L1_xattn_in['ln2_w'], 'L1_xattn_ln2_b': _L1_xattn_in['ln2_b']}

def reference(x, ctx_1024, mask_Bx1xSxS2_bk0, mask_Bx1xSxS2_bf1, L0_xattn_sWq, L0_xattn_sbq, L0_xattn_sWk, L0_xattn_sbk, L0_xattn_sWv, L0_xattn_sbv, L0_xattn_sWo, L0_xattn_sbo, L0_xattn_cWq, L0_xattn_cbq, L0_xattn_cWk, L0_xattn_cbk, L0_xattn_cWv, L0_xattn_cbv, L0_xattn_cWo, L0_xattn_cbo, L0_xattn_W1, L0_xattn_b1, L0_xattn_W2, L0_xattn_b2, L1_xattn_Wk, L1_xattn_bk, L1_xattn_Wv, L1_xattn_bv, L1_xattn_Wo, L1_xattn_bo, L1_xattn_gammas, L1_xattn_ln1_w, L1_xattn_ln1_b, L1_xattn_W1, L1_xattn_b1, L1_xattn_W2, L1_xattn_b2, L1_xattn_ln2_w, L1_xattn_ln2_b):
    import jax
    import jax.numpy as jnp

    def _L0_xattn_ref(tgt, encoder_out, tgt_mask, src_tgt_mask, sWq, sbq, sWk, sbk, sWv, sbv, sWo, sbo, cWq, cbq, cWk, cbk, cWv, cbv, cWo, cbo, W1, b1, W2, b2):
        import jax, jax.numpy as jnp
        import numpy as np
        import math
        B, L, D, H, DFF = (2, 256, 128, 16, 512)

        def _mha(xq, xkv, Wq, bq, Wk, bk, Wv, bv, Wo, bo, mask, h):
            b, lq, d = xq.shape
            dk = d // h
            q = (xq @ Wq + bq).reshape(b, lq, h, dk).transpose(0, 2, 1, 3)
            k = (xkv @ Wk + bk).reshape(b, -1, h, dk).transpose(0, 2, 1, 3)
            v = (xkv @ Wv + bv).reshape(b, -1, h, dk).transpose(0, 2, 1, 3)
            scores = jnp.einsum('bhqd,bhkd->bhqk', q, k) / jnp.sqrt(jnp.float32(dk))
            scores = jnp.where(mask, scores, jnp.float32(-1000000000.0))
            prob = jax.nn.softmax(scores, axis=-1)
            out = jnp.einsum('bhqk,bhkd->bhqd', prob, v)
            out = out.transpose(0, 2, 1, 3).reshape(b, lq, d)
            return out @ Wo + bo
        x = tgt + _mha(tgt, tgt, sWq, sbq, sWk, sbk, sWv, sbv, sWo, sbo, tgt_mask, H)
        x = x + _mha(x, encoder_out, cWq, cbq, cWk, cbk, cWv, cbv, cWo, cbo, src_tgt_mask, H)
        x = x + (jax.nn.relu(x @ W1 + b1) @ W2 + b2)
        return x

    def _L1_xattn_ref(query, key, values, Wk, bk, Wv, bv, Wo, bo, gammas, ln1_w, ln1_b, W1, b1, W2, b2, ln2_w, ln2_b, mask):
        import jax, jax.numpy as jnp
        import numpy as np
        NEG = -1e+32
        EPS_LN = 1e-05

        def _layer_norm(x, w, b):
            mu = jnp.mean(x, axis=-1, keepdims=True)
            var = jnp.mean((x - mu) ** 2, axis=-1, keepdims=True)
            return (x - mu) / jnp.sqrt(var + EPS_LN) * w + b

        def _forward(query, key, values, Wk, bk, Wv, bv, Wo, bo, gammas, ln1_w, ln1_b, W1, b1, W2, b2, ln2_w, ln2_b, mask):
            B, S, D = query.shape
            H = gammas.shape[0]
            dk = D // H

            def proj(x, W, b):
                return (x @ W.T + b).reshape(B, S, H, dk).transpose(0, 2, 1, 3)
            q = proj(query, Wk, bk)
            k = proj(key, Wk, bk)
            v = proj(values, Wv, bv)
            scores = jnp.einsum('bhqd,bhkd->bhqk', q, k) / np.sqrt(dk).astype(np.float32)
            allow = jnp.tril(jnp.ones((S, S), bool), k=mask - 1)[None, None]
            scores_ = jax.nn.softmax(jnp.where(allow, scores, NEG), axis=-1)
            scores_ = scores_ * allow.astype(scores_.dtype)
            distcum = jnp.cumsum(scores_, axis=-1)
            disttotal = jnp.sum(scores_, axis=-1, keepdims=True)
            idx = jnp.arange(S)
            position_effect = jnp.abs(idx[:, None] - idx[None, :]).astype(jnp.float32)[None, None]
            dist_scores = jnp.sqrt(jnp.clip((disttotal - distcum) * position_effect, 0.0, None))
            gamma = -jax.nn.softplus(gammas)[None]
            total_effect = jnp.clip(jnp.exp(dist_scores * gamma), 1e-05, 100000.0)
            total_effect = jax.lax.stop_gradient(total_effect)
            scores = scores * total_effect
            scores = jnp.where(allow, scores, NEG)
            attn = jax.nn.softmax(scores, axis=-1)
            out = jnp.einsum('bhqk,bhkd->bhqd', attn, v)
            concat = out.transpose(0, 2, 1, 3).reshape(B, S, D)
            query2 = concat @ Wo.T + bo
            x = _layer_norm(query + query2, ln1_w, ln1_b)
            ff = jax.nn.relu(x @ W1.T + b1) @ W2.T + b2
            x = _layer_norm(x + ff, ln2_w, ln2_b)
            return x
        return _forward(query, key, values, Wk, bk, Wv, bv, Wo, bo, gammas, ln1_w, ln1_b, W1, b1, W2, b2, ln2_w, ln2_b, mask)
    x = _L0_xattn_ref(x, ctx_1024, mask_Bx1xSxS2_bk0, mask_Bx1xSxS2_bf1, L0_xattn_sWq, L0_xattn_sbq, L0_xattn_sWk, L0_xattn_sbk, L0_xattn_sWv, L0_xattn_sbv, L0_xattn_sWo, L0_xattn_sbo, L0_xattn_cWq, L0_xattn_cbq, L0_xattn_cWk, L0_xattn_cbk, L0_xattn_cWv, L0_xattn_cbv, L0_xattn_cWo, L0_xattn_cbo, L0_xattn_W1, L0_xattn_b1, L0_xattn_W2, L0_xattn_b2)
    x = _L1_xattn_ref(x, ctx_1024, ctx_1024, L1_xattn_Wk, L1_xattn_bk, L1_xattn_Wv, L1_xattn_bv, L1_xattn_Wo, L1_xattn_bo, L1_xattn_gammas, L1_xattn_ln1_w, L1_xattn_ln1_b, L1_xattn_W1, L1_xattn_b1, L1_xattn_W2, L1_xattn_b2, L1_xattn_ln2_w, L1_xattn_ln2_b, 1)
    return x

_drawn_inputs = setup_inputs


def setup_inputs(seed=0):
    import zlib

    import numpy as np

    out = dict(_drawn_inputs(seed))
    spreads = {'L0_xattn_sbq': (0.0, 2.0),
     'L0_xattn_sbk': (0.0, 2.0),
     'L0_xattn_sbv': (0.0, 0.378),
     'L0_xattn_sbo': (0.0, 0.1),
     'L0_xattn_cbq': (0.0, 2.0),
     'L0_xattn_cbk': (0.0, 2.0),
     'L0_xattn_cbv': (0.0, 0.383),
     'L0_xattn_cbo': (0.0, 0.1),
     'L0_xattn_b1': (0.0, 0.299),
     'L0_xattn_b2': (0.0, 0.1),
     'L1_xattn_bk': (0.0, 2.0),
     'L1_xattn_bv': (0.0, 0.368),
     'L1_xattn_bo': (0.0, 0.1),
     'L1_xattn_ln1_w': (1.0, 0.2),
     'L1_xattn_ln1_b': (0.0, 0.1),
     'L1_xattn_b1': (0.0, 0.274),
     'L1_xattn_b2': (0.0, 0.1),
     'L1_xattn_ln2_w': (1.0, 0.2),
     'L1_xattn_ln2_b': (0.0, 0.1)}
    factors = {'L0_xattn_sWq': 8.0,
     'L0_xattn_sWk': 8.0,
     'L0_xattn_cWq': 8.0,
     'L0_xattn_cWk': 8.0,
     'L1_xattn_Wk': 8.0,
     'L1_xattn_gammas': 79.874}
    for name, (base, spread) in spreads.items():
        noise = np.random.default_rng([zlib.crc32(name.encode()), seed]).standard_normal(out[name].shape)
        drawn = base * np.exp(spread * noise) if base else spread * noise
        out[name] = jnp.asarray(drawn.astype(out[name].dtype))
    for name, factor in factors.items():
        out[name] = (out[name] * factor).astype(out[name].dtype)
    return out
```

```python
import concourse.bass as bass
from concourse import mybir
from contextlib import ExitStack

P = 128
NB, SEQ, D, H, DK, DFF = 128, 64, 128, 16, 8, 512
PAIRS = 4
TOK = PAIRS * P
GROUPS = NB * SEQ // TOK
HH = H // 2
HALF = HH * SEQ
CHUNKS = DFF // P
VW = 2 * (DK + 1)
W_COLS = {}
_at = 0
for _n, _w in (("q0", D), ("k0", D), ("v0", D), ("o0", D), ("q1", D), ("k1", D), ("v1", D), ("o1", D),
               ("w1_0", DFF), ("w2_0", DFF), ("q2", D), ("v2", D), ("o2", D), ("w1_1", DFF), ("w2_1", DFF)):
    W_COLS[_n] = (_at, _at + _w)
    _at += _w
W_TOTAL = _at
VECS = ["bq0", "bk0", "bv0", "bo0", "bq1", "bk1", "bv1", "bo1", "b2_0", "bk2", "bv2", "bo2", "ln1_w", "ln1_b",
        "b2_1", "b1_0_0", "b1_0_1", "b1_0_2", "b1_0_3", "b1_1_0", "b1_1_1", "b1_1_2", "b1_1_3"]
C_IDENT, C_HEAD, C_CAUSAL, C_DIST, C_CARRY, C_VONE = 0, 128, 136, 200, 264, 1288
C_TOTAL = C_VONE + HH * VW
NEG0, NEG1, EPS = -1.0e9, -1.0e32, 1.0e-5
TINY = 1.0e-18
SCALE = float(DK) ** -0.5

L1_SLOTS = (0, 2, 4, 6)


def iteration_order(l0, l1):
    out = []
    if l1:
        out += [("K", 2), ("V", 2), ("Q", 2), ("KM", 2)]
    if l0:
        out += [("XT",), ("CT",), ("MASK",), ("K", 0), ("Q", 0), ("V", 0), ("KM", 0)]
    scores = {}
    for k, fp in enumerate([(0, 0), (0, 1), (0, 2), (0, 3), None, (1, 0), (1, 1), (1, 2), (1, 3), None, None]):
        if fp:
            scores[k] = fp
    trans = {k + 1: fp for k, fp in scores.items()}
    for k in range(11):
        new, old = scores.get(k), trans.get(k)
        r1 = L1_SLOTS.index(k) if k in L1_SLOTS else None
        r2 = L1_SLOTS.index(k - 1) if k - 1 in L1_SLOTS else None
        r3 = L1_SLOTS.index(k - 2) if k - 2 in L1_SLOTS else None
        r4 = L1_SLOTS.index(k - 3) if k - 3 in L1_SLOTS else None
        if l0 and new:
            out += [("S",) + new, ("D1",) + new, ("SUB",) + new]
        if l1 and r2 is not None:
            out += [("D2", 2, r2), ("PM", 2, r2)]
        if l1 and r1 is not None:
            out += [("S", 2, r1), ("D1", 2, r1), ("SUB", 2, r1), ("E1", 2, r1)]
        if l1 and r3 is not None:
            out += [("D3", 2, r3), ("SUB2", 2, r3)]
        if l0 and old:
            out += [("T",) + old, ("PX",) + old]
        if l1 and r4 is not None:
            out += [("T", 2, r4), ("PX", 2, r4)]
        if l1 and r2 is not None:
            out += [("LG", 2, r2)]
        if l0 and k == 2:
            out += [("K", 1), ("V", 1), ("KM", 1)]
        if l0 and old:
            out += [("PV",) + old, ("N",) + old]
        if l1 and r4 is not None:
            out += [("PV", 2, r4), ("N", 2, r4)]
        if l0 and k in (4, 9):
            f = 0 if k == 4 else 1
            out += [("OT", f), ("OP", f)]
            if f == 0:
                out += [("Q", 1)]
    if l1:
        out += [("OT", 2), ("OP", 2), ("LN", 0)]
    if l0:
        out += [("H", 0, c) for c in range(CHUNKS)]
    if l1:
        out += [("X2T",)]
        out += [("H", 1, c) for c in range(CHUNKS)]
    if l0:
        out += [("Y0",), ("XLB",)]
    if l1:
        out += [("Y1",), ("LN", 1), ("OUT",)]
    return out


MISC_USES = {"XT", "CT", "K", "Q", "V", "OT", "OP", "X2T", "H", "Y0", "Y1"}
SEGMENTS = [iteration_order(True, False), iteration_order(True, True), iteration_order(False, True)]


class Turns:

    def __init__(self, kinds):
        self.lists = [[s for s in seg if s[0] in kinds] for seg in SEGMENTS]

    def at(self, seg, i, stage):
        first, loop, last = self.lists
        k = self.lists[seg].index(stage)
        if seg == 0:
            return k, 0, 0
        if seg == 1:
            return len(first) + k, len(loop), i - 1
        return len(first) + (GROUPS - 1) * len(loop) + k, 0, 0

    def number(self, seg, i, stage):
        c, n, j = self.at(seg, i, stage)
        return c + j * n if n else c

    def before(self, seg, i):
        first, loop, _ = self.lists
        return 0 if seg == 0 else len(first) + (i - 1) * len(loop)

    def slot(self, seg, i, stage, slots):
        c, n, _ = self.at(seg, i, stage)
        assert n % slots == 0
        return c % slots

    def turn_of_slot(self, seg, i, stage, slots):
        c, n, j = self.at(seg, i, stage)
        return c // slots + j * (n // slots) if n else c // slots


PAIR_SCORES = Turns({"S"})
PAIR_TAILS = Turns({"T"})
MISC = Turns(MISC_USES)


def count(value):
    return max(value, 0) if isinstance(value, int) else value


def build(nc, x, ctx_in, mask0, mask1, weights, vecs, rows, gam, consts, out):
    F32, U8 = mybir.dt.float32, mybir.dt.uint8
    ALU, ACT, AX = mybir.AluOpType, mybir.ActivationFunctionType, mybir.AxisListType

    with ExitStack() as ctx:
        def sb(name, shape, dt=F32):
            return ctx.enter_context(nc.sbuf_tensor(name, [P] + shape, dt))

        def sem(name):
            return ctx.enter_context(nc.semaphore(name))

        def sems(name, n):
            return [sem(f"{name}{k}") for k in range(n)]

        W = sb("W", [W_TOTAL])
        V = sb("V", [len(VECS)])
        ln2 = sb("ln2", [2, D])
        const = sb("const", [C_TOTAL])
        gamma2 = sb("gamma2", [H])
        gtmp = sb("gtmp", [4, H])
        bqs = sb("bqs", [3])
        bln = sb("bln", [1])
        epsc = sb("epsc", [2])
        ident = const[:, C_IDENT:C_IDENT + P]
        head_rows = const[:, C_HEAD:C_HEAD + HH]
        causal = const[:, C_CAUSAL:C_CAUSAL + SEQ]
        distance = const[:, C_DIST:C_DIST + SEQ]
        carry = const[:, C_CARRY:C_CARRY + 2 * HALF]
        vone = const[:, C_VONE:C_VONE + HH * VW]

        def w(name):
            return W[:, W_COLS[name][0]:W_COLS[name][1]]

        def vec(name):
            k = VECS.index(name)
            return V[:, k:k + 1]

        xin = sb("xin", [PAIRS, D])
        cin = sb("cin", [PAIRS, D])
        min_ = [sb(f"mask_in{f}", [PAIRS, SEQ], U8) for f in range(2)]
        bias = [sb(f"mask_bias{f}", [PAIRS, SEQ]) for f in range(2)]
        some = [sb(f"some_key{f}", [PAIRS]) for f in range(2)]
        xA, xB, xF, xL, xLb, cT = (sb(n, [TOK]) for n in ("xA", "xB", "xF", "xL", "xLb", "cT"))
        x2T, x2bT = sb("x2T", [TOK]), sb("x2bT", [TOK])
        qT = [sb(f"qT{f}", [TOK]) for f in range(3)]
        kT = [sb(f"kT{f}", [TOK]) for f in range(3)]
        vb = [sb(f"vb{f}", [2 * PAIRS, HH, VW]) for f in range(3)]
        oT = [sb(f"oT{f}", [TOK]) for f in range(3)]
        hT = [sb(f"hT{l}", [CHUNKS, TOK]) for l in range(2)]
        on = [sb(f"on{l}", [PAIRS, D]) for l in range(2)]
        xn = sb("xn", [2, PAIRS, D])
        yo = sb("yo", [PAIRS, D])
        st6 = sb("st6", [2, PAIRS, 6])
        mv = sb("mv", [2, PAIRS, 2])
        rstd = sb("rstd", [2, PAIRS])
        lnv = sb("lnv", [2, PAIRS])
        km = [sb(f"km{f}", [HH, TOK]) for f in range(3)]
        sm = [sb("sm0", [2, 2, HALF]), sb("sm1", [2, 2, HALF])]
        mx = [sb("mx0", [2, 2, HH]), sb("mx1", [2, 2, HH])]
        mx2 = sb("mx2", [2, 2, HH])
        ss = sb("ss", [2, HH, 2, SEQ])
        pt = sb("pt", [2, HH, P])
        ex = sb("ex", [H, SEQ])
        suf = sb("suf", [H, SEQ])
        wd = sb("wd", [H, SEQ])
        te = sb("te", [2, H, SEQ])
        rtot = sb("rtot", [2, H])
        cc = sb("cc", [2, H])
        rz = sb("rz", [2, H])

        s_ps = [ctx.enter_context(nc.psum_tensor(f"s_ps{n}", [P, 512], F32)) for n in range(3)]
        t_ps = [ctx.enter_context(nc.psum_tensor(f"t_ps{n}", [P, 512], F32)) for n in range(2)]
        o_ps = ctx.enter_context(nc.psum_tensor("o_ps", [P, 512], F32))
        m_ps = [ctx.enter_context(nc.psum_tensor(f"m_ps{n}", [P, 512], F32)) for n in range(2)]

        const_loaded = sem("const_loaded")
        x_loaded, c_loaded, mask_loaded = sem("x_loaded"), sem("c_loaded"), sem("mask_loaded")
        setup_act, setup_dve, setup_pool = sem("setup_act"), sem("setup_dve"), sem("setup_pool")
        misc_ready = sems("misc_ready", 2)
        misc_left = sems("misc_left", 2)
        bias_done = sem("bias_done")
        km_ready = sems("km_ready", 3)
        scores_ready = sem("scores_ready")
        scores_left = sem("scores_left")
        max_ready = sems("max_ready", 2)
        sub_done = sems("sub_done", 2)
        exp1_done, scan_done, cc_ready = sem("exp1_done"), sem("scan_done"), sem("cc_ready")
        rtot_done = sem("rtot_done")
        dist_done, scaled_done = sem("dist_done"), sem("scaled_done")
        ln_done, root_done, effect_ready = sem("ln_done"), sem("root_done"), sem("effect_ready")
        s2_done, max2_ready, sub2_done = sem("s2_done"), sem("max2_ready"), sem("sub2_done")
        shifted_t = sem("shifted_t")
        probs_ready = sem("probs_ready")
        pv_done = sem("pv_done")
        rz_done, norm_done = sem("rz_done"), sem("norm_done")
        xlb_done = sem("xlb_done")
        stats_done, mean_ready = sem("stats_done"), sem("mean_ready")
        lnv_done, rstd_ready = sem("lnv_done"), sem("rstd_ready")
        gain_done, y_ready, stored = sem("gain_done"), sem("y_ready"), sem("stored")

        xv = x.rearrange("(n p) d -> p n d", p=P)
        cv = ctx_in.rearrange("(n p) d -> p n d", p=P)
        mv0 = mask0.rearrange("(n p) k -> p n k", p=P)
        mv1 = mask1.rearrange("(n p) k -> p n k", p=P)
        ov = out.rearrange("(n p) d -> p n d", p=P)

        def layer(f):
            return 1 if f == 2 else 0

        def pair_no(f, p, i):
            return (i - 1) * PAIRS + p if f == 2 else i * 2 * PAIRS + f * PAIRS + p

        def group_no(f, i):
            return i - 1 if f == 2 else i

        def pair_slot(f, p, n):
            return (p if f == 2 else f * PAIRS + p) % n

        def sm_slot(seg, f, p):
            return p % 2 if f == 2 else pair_slot(f, p, 2)

        def run(eng, body):
            body(0, 0)
            with eng.Fori(1, GROUPS) as i:
                body(1, i)
            body(2, GROUPS)

        def misc(seg, i, stage):
            return MISC.slot(seg, i, stage, 2), MISC.turn_of_slot(seg, i, stage, 2)

        def left(seg, i, stage):
            b, n = misc(seg, i, stage)
            return misc_left[b], n + 1

        def written(seg, i, stage):
            b, n = misc(seg, i, stage)
            return misc_ready[b], n + 1

        block = ctx.enter_context(nc.Block())

        @block.sync
        def _(sp):
            sp.dma_start(const[:, :], consts).then_inc(const_loaded, 16)
            sp.dma_start(W[:, :], weights).then_inc(const_loaded, 16)
            sp.dma_start(V[:, :], vecs).then_inc(const_loaded, 16)
            sp.dma_start(gtmp[:, 0, :], gam).then_inc(const_loaded, 16)
            sp.dma_start(ln2[:, :, :], rows).then_inc(stored, 16)

            def load(g):
                sp.dma_start(xin[:, :, :], xv[:, bass.ds(g * PAIRS, PAIRS), :]).then_inc(x_loaded, 16)
                sp.dma_start(cin[:, :, :], cv[:, bass.ds(g * PAIRS, PAIRS), :]).then_inc(c_loaded, 16)
                sp.dma_start(min_[0][:, :, :], mv0[:, bass.ds(g * PAIRS, PAIRS), :]).then_inc(mask_loaded, 16)
                sp.dma_start(min_[1][:, :, :], mv1[:, bass.ds(g * PAIRS, PAIRS), :]).then_inc(mask_loaded, 16)

            load(0)

            def load_next(seg, i):
                b, n = misc(seg, i, ("XT",))
                sp.wait_ge(misc_ready[b], n + 1)
                b, n = misc(seg, i, ("CT",))
                sp.wait_ge(misc_ready[b], n + 1)
                sp.wait_ge(bias_done, 4 * (i + 1))
                load(i + 1)

            def store(i):
                sp.wait_ge(y_ready, i + 1)
                sp.dma_start(ov[:, bass.ds((i - 1) * PAIRS, PAIRS), :], yo[:, :, :]).then_inc(stored, 16)

            load_next(0, 0)
            with sp.Fori(1, GROUPS - 1) as i:
                load_next(1, i)
                store(i)
            store(GROUPS - 1)
            store(GROUPS)
            sp.wait_ge(stored, 16 * (GROUPS + 1))

        @block.tensor
        def _(pe):
            mm, tr = nc.tensor.matmul, nc.tensor.transpose
            pe.wait_ge(const_loaded, 64)

            def take(seg, i, stage):
                b, n = misc(seg, i, stage)
                pe.wait_ge(misc_left[b], n)
                return b

            def body(seg, i):
                for stage in SEGMENTS[seg]:
                    kind = stage[0]
                    if kind in ("XT", "CT"):
                        b = take(seg, i, stage)
                        pe.wait_ge(x_loaded if kind == "XT" else c_loaded, 16 * (i + 1))
                        src = xin if kind == "XT" else cin
                        for j in range(PAIRS):
                            last = tr(m_ps[b][:, j * P:(j + 1) * P], src[:, j, :], ident)
                        last.then_inc(misc_ready[b], 1)
                    elif kind in ("Q", "K"):
                        f = stage[1]
                        b = take(seg, i, stage)
                        if f == 0:
                            pe.wait_ge(*left(seg, i, ("XT",)))
                        elif kind == "K" and f == 1:
                            pe.wait_ge(*left(seg, i, ("CT",)))
                        elif kind == "Q" and f == 1:
                            pe.wait_ge(*left(seg, i, ("OP", 0)))
                        elif kind == "Q" and f == 2:
                            pe.wait_ge(xlb_done, i)
                        src = {("Q", 0): xA, ("K", 0): xA, ("Q", 1): xB, ("K", 1): cT, ("Q", 2): xL,
                               ("K", 2): cT}[kind, f]
                        wt = w("q2") if f == 2 else w(f"{kind.lower()}{f}")
                        mm(m_ps[b][:, :], wt, src[:, :], start=True, stop=True).then_inc(misc_ready[b], 1)
                    elif kind == "V":
                        f = stage[1]
                        b = take(seg, i, stage)
                        src = xA if f == 0 else cT
                        wv = w(f"v{f}")
                        for n in range(2 * PAIRS):
                            for g in range(2):
                                last = mm(m_ps[b][64 * g:64 * g + 64, n * 64:(n + 1) * 64],
                                          src[:, n * SEQ:(n + 1) * SEQ], wv[:, 64 * g:64 * g + 64],
                                          start=True, stop=True)
                        last.then_inc(misc_ready[b], 1)
                    elif kind == "S":
                        _, f, p = stage
                        l, u = layer(f), pair_no(f, p, i)
                        n = PAIR_SCORES.number(seg, i, stage)
                        if p == 0:
                            pe.wait_ge(*left(seg, i, ("Q", f)))
                            pe.wait_ge(km_ready[f], group_no(f, i) + 1)
                        c, per, _ = PAIR_SCORES.at(seg, i, stage)
                        for g in range(2):
                            bank = (2 * c + g) % 3
                            assert (2 * per) % 3 == 0
                            pe.wait_ge(scores_left, count(2 * n + g - 2))
                            pe.nop(nofuse=True)
                            pe.nop(nofuse=True)
                            for s in range(2):
                                t0 = (2 * p + s) * SEQ
                                last = mm(s_ps[bank][64 * s:64 * s + 64, :], qT[f][64 * g:64 * g + 64, t0:t0 + SEQ],
                                          km[f][64 * g:64 * g + 64, :, t0:t0 + SEQ],
                                          start=True, stop=True)
                            last.then_inc(scores_ready, 1)
                    elif kind == "T":
                        _, f, p = stage
                        u = pair_no(f, p, i)
                        t = PAIR_TAILS.number(seg, i, stage)
                        slot = PAIR_TAILS.slot(seg, i, stage, 2)
                        if f == 2:
                            pe.wait_ge(sub2_done, u + 1)
                        else:
                            pe.wait_ge(sub_done[0], 2 * u + 2)
                        for q in range(2):
                            pe.wait_ge(probs_ready, count(2 * t - 1 + q))
                            for j in range(4):
                                last = tr(t_ps[q][:, j * P:(j + 1) * P], ss[:, slot, 4 * q + j, :, :], ident)
                            last.then_inc(shifted_t, 1)
                    elif kind == "PV":
                        _, f, p = stage
                        t = PAIR_TAILS.number(seg, i, ("T", f, p))
                        slot = PAIR_TAILS.slot(seg, i, ("T", f, p), 2)
                        if p == 0:
                            pe.wait_ge(*left(seg, i, ("V", f)))
                        pe.wait_ge(norm_done, t)
                        for q in range(2):
                            pe.wait_ge(probs_ready, 2 * t + 1 + q)
                            for hh in range(4 * q, 4 * q + 4):
                                for s in range(2):
                                    last = mm(o_ps[64 * s:64 * s + 64, hh * VW:(hh + 1) * VW],
                                              pt[:, slot, hh, 64 * s:64 * s + 64], vb[f][:, 2 * p + s, hh, :],
                                              start=True, stop=True)
                        last.then_inc(pv_done, 1)
                    elif kind == "OT":
                        f = stage[1]
                        b = take(seg, i, stage)
                        pe.wait_ge(norm_done, PAIR_TAILS.number(seg, i, ("T", f, PAIRS - 1)) + 1)
                        for j in range(PAIRS):
                            last = tr(m_ps[b][:, j * P:(j + 1) * P], on[layer(f)][:, j, :], ident)
                        last.then_inc(misc_ready[b], 1)
                    elif kind == "OP":
                        f = stage[1]
                        b = take(seg, i, stage)
                        pe.wait_ge(*left(seg, i, ("OT", f)))
                        if f < 2:
                            last = mm(m_ps[b][:, :], w(f"o{f}"), oT[f][:, :], start=True, stop=True)
                        else:
                            pe.wait_ge(xlb_done, i)
                            for j in range(PAIRS):
                                o = m_ps[b][:, j * P:(j + 1) * P]
                                mm(o, xLb[:, j * P:(j + 1) * P], ident, start=True, stop=False)
                                last = mm(o, oT[f][:, j * P:(j + 1) * P], w("o2"), start=False, stop=True)
                        last.then_inc(misc_ready[b], 1)
                    elif kind == "X2T":
                        b = take(seg, i, stage)
                        pe.wait_ge(*left(seg, i, ("OP", 2)))
                        for j in range(PAIRS):
                            last = tr(m_ps[b][:, j * P:(j + 1) * P], xn[:, 0, j, :], ident)
                        last.then_inc(misc_ready[b], 1)
                    elif kind == "H":
                        _, l, c = stage
                        b = take(seg, i, stage)
                        pe.wait_ge(*left(seg, i, ("X2T",) if l else ("OP", 1)))
                        mm(m_ps[b][:, :], w(f"w1_{l}")[:, c * P:(c + 1) * P], (x2T if l else xF)[:, :],
                           start=True, stop=True).then_inc(misc_ready[b], 1)
                    elif kind == "Y0":
                        b = take(seg, i, stage)
                        for c in range(CHUNKS):
                            pe.wait_ge(*left(seg, i, ("H", 0, c)))
                            last = mm(m_ps[b][:, :], w("w2_0")[:, c * P:(c + 1) * P], hT[0][:, c, :],
                                      start=c == 0, stop=c == CHUNKS - 1)
                        last.then_inc(misc_ready[b], 1)
                    elif kind == "Y1":
                        b = take(seg, i, stage)
                        for c in range(CHUNKS):
                            pe.wait_ge(*left(seg, i, ("H", 1, c)))
                        for j in range(PAIRS):
                            o = m_ps[b][:, j * P:(j + 1) * P]
                            mm(o, x2bT[:, j * P:(j + 1) * P], ident, start=True, stop=False)
                            for c in range(CHUNKS):
                                last = mm(o, hT[1][:, c, j * P:(j + 1) * P], w("w2_1")[:, c * P:(c + 1) * P],
                                          start=False, stop=c == CHUNKS - 1)
                        last.then_inc(misc_ready[b], 1)

            run(pe, body)

        @block.scalar
        def _(act):
            A = nc.scalar.activation
            nc.scalar.preload_act_table_set("natural_log_exp_and_others")
            act.wait_ge(const_loaded, 64)
            act.wait_ge(setup_dve, 1)
            A(gtmp[:, 2, :], gtmp[:, 1, :], ACT.Exp, scale=-1.0).then_inc(setup_act, 1)
            act.wait_ge(setup_act, 1)
            A(gtmp[:, 3, :], gtmp[:, 2, :], ACT.Ln, bias=1.0).then_inc(setup_act, 1)
            act.wait_ge(setup_dve, 6)

            def evac(seg, i, stage, dst, func, **kw):
                b, n = misc(seg, i, stage)
                act.wait_ge(misc_ready[b], n + 1)
                A(dst, m_ps[b][:, :], func, **kw).then_inc(misc_left[b], 1)

            def body(seg, i):
                for stage in SEGMENTS[seg]:
                    kind = stage[0]
                    if kind == "XT":
                        evac(seg, i, stage, xA[:, :], ACT.Copy)
                    elif kind == "CT":
                        evac(seg, i, stage, cT[:, :], ACT.Copy)
                    elif kind == "Q":
                        evac(seg, i, stage, qT[stage[1]][:, :], ACT.Identity, bias=bqs[:, stage[1]:stage[1] + 1],
                             scale=SCALE)
                    elif kind == "K":
                        evac(seg, i, stage, kT[stage[1]][:, :], ACT.Identity, bias=vec(f"bk{stage[1]}"))
                    elif kind == "V":
                        f = stage[1]
                        b, n = misc(seg, i, stage)
                        act.wait_ge(misc_ready[b], n + 1)
                        if f == 0:
                            act.wait_ge(setup_pool, 3)
                        for g in range(2):
                            last = A(vb[f][64 * g:64 * g + 64, :, :, 9 * g:9 * g + DK],
                                     m_ps[b][64 * g:64 * g + 64, :].rearrange("p (n h d) -> p n h d", h=HH, d=DK),
                                     ACT.Copy)
                        last.then_inc(misc_left[b], 1)
                    elif kind == "E1":
                        u = pair_no(2, stage[2], i)
                        e = ex[:, :, :]
                        act.wait_ge(sub_done[1], 2 * u + 2)
                        A(e, e, ACT.Exp).then_inc(exp1_done, 1)
                    elif kind == "LG":
                        p = stage[2]
                        u = pair_no(2, p, i)
                        slot = pair_slot(2, p, 2)
                        t = te[:, slot, :, :]
                        act.wait_ge(scaled_done, u + 1)
                        if p:
                            act.wait_ge(sub2_done, count(u - 1))
                        A(t, wd[:, :, :], ACT.Ln, bias=epsc[:, 1:2]).then_inc(ln_done, 1)
                        act.wait_ge(ln_done, u + 1)
                        A(t, t, ACT.Exp, scale=0.5).then_inc(root_done, 1)
                        act.wait_ge(root_done, u + 1)
                        A(t, t, ACT.Exp, scale=-1.0).then_inc(effect_ready, 1)
                    elif kind == "PX":
                        _, f, p = stage
                        t = PAIR_TAILS.number(seg, i, ("T", f, p))
                        slot = PAIR_TAILS.slot(seg, i, ("T", f, p), 2)
                        act.wait_ge(pv_done, count(t - 1))
                        for q in range(2):
                            act.wait_ge(shifted_t, 2 * t + q + 1)
                            A(pt[:, slot, 4 * q:4 * q + 4, :], t_ps[q][:, :].rearrange("p (h t) -> p h t", h=4),
                              ACT.Exp).then_inc(probs_ready, 1)
                    elif kind == "OT":
                        evac(seg, i, stage, oT[stage[1]][:, :], ACT.Identity, bias=vec(f"bv{stage[1]}"))
                    elif kind == "X2T":
                        b, n = misc(seg, i, stage)
                        act.wait_ge(misc_ready[b], n + 1)
                        A(x2T[:, :], m_ps[b][:, :], ACT.Identity, bias=vec("ln1_b"), scale=vec("ln1_w"))
                        A(x2bT[:, :], m_ps[b][:, :], ACT.Identity, bias=bln[:, 0:1],
                          scale=vec("ln1_w")).then_inc(misc_left[b], 1)
                    elif kind == "H":
                        _, l, c = stage
                        evac(seg, i, stage, hT[l][:, c, :], ACT.Relu, bias=vec(f"b1_{l}_{c}"))
                    elif kind == "LN":
                        l = stage[1]
                        n = (i - 1) * 2 + l
                        act.wait_ge(mean_ready, n + 1)
                        A(lnv[:, l, :], mv[:, l, :, 1], ACT.Ln, bias=epsc[:, 0:1]).then_inc(lnv_done, 1)
                        act.wait_ge(lnv_done, n + 1)
                        A(rstd[:, l, :], lnv[:, l, :], ACT.Exp, scale=-0.5).then_inc(rstd_ready, 1)

            run(act, body)

        @block.vector
        def _(dve):
            v = nc.vector
            dve.wait_ge(const_loaded, 64)
            v.scalar_tensor_tensor(gtmp[:, 1, :], gtmp[:, 0, :], -1.0, gtmp[:, 0, :], ALU.mult,
                                   ALU.max).then_inc(setup_dve, 1)
            for f, name in enumerate(("bq0", "bq1", "bk2")):
                v.tensor_scalar(bqs[:, f:f + 1], vec(name), SCALE, None, ALU.mult).then_inc(setup_dve, 1)
            v.memset(epsc[:, 0:1], EPS)
            v.memset(epsc[:, 1:2], TINY).then_inc(setup_dve, 1)
            v.tensor_tensor(bln[:, :], vec("ln1_b"), vec("b2_1"), ALU.add).then_inc(setup_dve, 1)
            dve.wait_ge(setup_act, 2)
            v.tensor_scalar(gtmp[:, 0, :], gtmp[:, 0, :], 0.0, None, ALU.max).then_inc(setup_dve, 1)
            dve.wait_ge(setup_dve, 7)
            v.tensor_tensor(gtmp[:, 1, :], gtmp[:, 0, :], gtmp[:, 3, :], ALU.add).then_inc(setup_dve, 1)
            dve.wait_ge(setup_dve, 8)
            v.tensor_tensor(gamma2[:, :], gtmp[:, 1, :], gtmp[:, 1, :], ALU.mult).then_inc(setup_dve, 1)
            dve.wait_ge(setup_dve, 9)

            def heads(ap):
                return ap.rearrange("p (h k) -> p h k", k=SEQ)

            def body(seg, i):
                for stage in SEGMENTS[seg]:
                    kind = stage[0]
                    if kind == "MASK":
                        dve.wait_ge(mask_loaded, 32 * (i + 1))
                        for f in range(2):
                            v.tensor_scalar(bias[f][:, :, :], min_[f][:, :, :], 1.0, -NEG0, ALU.subtract,
                                            ALU.mult).then_inc(bias_done, 1)
                            v.tensor_reduce(out=some[f][:, :], in_=min_[f][:, :, :], op=ALU.max,
                                            axis=AX.X).then_inc(bias_done, 1)
                    elif kind == "KM":
                        f = stage[1]
                        dve.wait_ge(*left(seg, i, ("K", f)))
                        for h in range(HH):
                            last = v.tensor_scalar(km[f][:, h, :], kT[f][:, :], head_rows[:, h:h + 1], None,
                                                   ALU.mult)
                        last.then_inc(km_ready[f], 1)
                    elif kind == "D1":
                        _, f, p = stage
                        l, u = layer(f), pair_no(f, p, i)
                        n = PAIR_SCORES.number(seg, i, ("S", f, p))
                        c, _, _ = PAIR_SCORES.at(seg, i, ("S", f, p))
                        slot = pair_slot(f, p, 2)
                        sslot = slot
                        if l == 0 and p == 0 and f == 0:
                            dve.wait_ge(bias_done, 4 * (i + 1))
                        if (f, p) != (2, 0):
                            dve.wait_ge(sub_done[l], count(2 * (u - 1)))
                        for g in range(2):
                            bank = s_ps[(2 * c + g) % 3]
                            dve.wait_ge(scores_ready, 2 * n + g + 1)
                            if l == 0:
                                v.scalar_tensor_tensor(heads(sm[0][:, sslot, g, :]), heads(bank[:, :]),
                                                       some[f][:, p:p + 1],
                                                       bias[f][:, None, p, :].broadcast_to([P, HH, SEQ]),
                                                       ALU.mult, ALU.add).then_inc(scores_left, 1)
                            else:
                                v.tensor_tensor(heads(sm[1][:, sslot, g, :]), heads(bank[:, :]),
                                                causal[:, None, :].broadcast_to([P, HH, SEQ]),
                                                ALU.add).then_inc(scores_left, 1)
                        for g in range(2):
                            dve.wait_ge(scores_left, 2 * n + g + 1)
                            v.tensor_reduce(out=mx[l][:, slot, g, :], in_=heads(sm[l][:, sslot, g, :]), op=ALU.max,
                                            axis=AX.X).then_inc(max_ready[l], 1)
                    elif kind == "D2":
                        p = stage[2]
                        u, slot = pair_no(2, p, i), pair_slot(2, p, 2)
                        dve.wait_ge(exp1_done, u + 1)
                        if p:
                            dve.wait_ge(dist_done, u)
                        flat = slice(H * SEQ - 1, None, -1)
                        v.tensor_tensor_scan(suf[:, :, :].rearrange("p h k -> p (h k)")[:, flat], carry[:, flat],
                                             ex[:, :, :].rearrange("p h k -> p (h k)")[:, flat], 0.0,
                                             ALU.mult, ALU.add).then_inc(scan_done, 1)
                        dve.wait_ge(scan_done, u + 1)
                        if p:
                            dve.wait_ge(scaled_done, count(u - 1))
                        v.reciprocal(rtot[:, slot, :], suf[:, :, 0]).then_inc(rtot_done, 1)
                        dve.wait_ge(rtot_done, u + 1)
                        v.tensor_tensor(cc[:, slot, :], gamma2[:, :], rtot[:, slot, :],
                                        ALU.mult).then_inc(cc_ready, 1)
                    elif kind == "D3":
                        p = stage[2]
                        u, slot = pair_no(2, p, i), pair_slot(2, p, 2)
                        t = te[:, slot, :, :].rearrange("p h k -> p (h k)")
                        dve.wait_ge(effect_ready, u + 1)
                        v.scalar_tensor_tensor(t, t, 1.0e-5, sm[1][:, slot, :, :].rearrange("p g c -> p (g c)"),
                                               ALU.max, ALU.mult).then_inc(s2_done, 1)
                        dve.wait_ge(s2_done, u + 1)
                        if p:
                            dve.wait_ge(sub2_done, count(u - 1))
                        v.tensor_reduce(out=mx2[:, slot, :, :].rearrange("p g h -> p (g h)"), in_=te[:, slot, :, :],
                                        op=ALU.max, axis=AX.X).then_inc(max2_ready, 1)
                    elif kind == "N":
                        _, f, p = stage
                        t = PAIR_TAILS.number(seg, i, ("T", f, p))
                        slot = PAIR_TAILS.slot(seg, i, ("T", f, p), 2)
                        o = o_ps[:, 0:HH * VW].rearrange("p (h g c) -> p g h c", h=HH, g=2)
                        z = rz[:, slot, :].rearrange("p (g h) -> p g h", g=2)
                        dve.wait_ge(pv_done, t + 1)
                        v.reciprocal(z, o[:, :, :, DK]).then_inc(rz_done, 1)
                        dve.wait_ge(rz_done, t + 1)
                        v.tensor_tensor(on[layer(f)][:, p, :].rearrange("p (g h d) -> p g h d", g=2, h=HH),
                                        o[:, :, :, 0:DK], z[:, :, :, None].broadcast_to([P, 2, HH, DK]),
                                        ALU.mult).then_inc(norm_done, 1)
                    elif kind == "OP" and stage[1] < 2:
                        f = stage[1]
                        b, n = misc(seg, i, stage)
                        dve.wait_ge(misc_ready[b], n + 1)
                        v.scalar_tensor_tensor((xB, xF)[f][:, :], m_ps[b][:, :], vec(f"bo{f}"), (xA, xB)[f][:, :],
                                               ALU.add, ALU.add).then_inc(misc_left[b], 1)
                    elif kind == "Y0":
                        b, n = misc(seg, i, stage)
                        dve.wait_ge(misc_ready[b], n + 1)
                        dve.wait_ge(xlb_done, i)
                        v.scalar_tensor_tensor(xL[:, :], m_ps[b][:, :], vec("b2_0"), xF[:, :],
                                               ALU.add, ALU.add).then_inc(misc_left[b], 1)
                    elif kind == "LN":
                        l = stage[1]
                        n = (i - 1) * 2 + l
                        src = ("Y1",) if l else ("OP", 2)
                        b, k = misc(seg, i, src)
                        dve.wait_ge(misc_ready[b], k + 1)
                        if l:
                            dve.wait_ge(y_ready, i)
                        for j in range(PAIRS):
                            v.bn_stats(st6[:, l, j, :], m_ps[b][:, j * P:(j + 1) * P]).then_inc(stats_done, 1)
                        for j in range(PAIRS):
                            dve.wait_ge(stats_done, n * PAIRS + j + 1)
                            dve.nop(nofuse=True)
                            dve.nop(nofuse=True)
                            last = v.bn_aggr(mv[:, l, j, :], st6[:, l, j, :])
                        last.then_inc(mean_ready, 1)
                        dve.wait_ge(rstd_ready, n + 1)
                        for j in range(PAIRS):
                            last = v.tensor_scalar(xn[:, l, j, :], m_ps[b][:, j * P:(j + 1) * P], mv[:, l, j, 0:1],
                                                   rstd[:, l, j:j + 1], ALU.subtract, ALU.mult)
                        last.then_inc(misc_left[b], 1)

            run(dve, body)

        @block.gpsimd
        def _(pool):
            g_ = nc.gpsimd
            pool.wait_ge(const_loaded, 64)
            for f in range(3):
                for n in range(2 * PAIRS):
                    last = g_.tensor_copy(vb[f][:, n, :, :].rearrange("p h c -> p (h c)"), vone)
                last.then_inc(setup_pool, 1)
            g_.memset(wd[:, :, SEQ - 1:SEQ], 0.0).then_inc(y_ready, 1)

            def body(seg, i):
                for stage in SEGMENTS[seg]:
                    kind = stage[0]
                    if kind == "SUB":
                        _, f, p = stage
                        l, u, slot = layer(f), pair_no(f, p, i), pair_slot(f, p, 2)
                        if l == 0:
                            t = PAIR_TAILS.number(seg, i, ("T", f, p))
                            pool.wait_ge(shifted_t, count(2 * t - 2))
                        elif p:
                            pool.wait_ge(scan_done, u)
                        for g in range(2):
                            pool.wait_ge(max_ready[l], 2 * u + g + 1)
                            dst = ss[:, PAIR_TAILS.slot(seg, i, ("T", f, p), 2), :, g, :] if l == 0 else \
                                ex[:, HH * g:HH * g + HH, :]
                            g_.tensor_tensor(dst, sm[l][:, slot, g, :].rearrange("p (h k) -> p h k", k=SEQ),
                                             mx[l][:, slot, g, :, None].broadcast_to([P, HH, SEQ]),
                                             ALU.subtract).then_inc(sub_done[l], 1)
                    elif kind == "PM":
                        p = stage[2]
                        u, slot = pair_no(2, p, i), pair_slot(2, p, 2)
                        pool.wait_ge(scan_done, u + 1)
                        if p:
                            pool.wait_ge(ln_done, u)
                        g_.tensor_tensor(wd[:, :, 0:SEQ - 1], suf[:, :, 1:SEQ],
                                         distance[:, None, 0:SEQ - 1].broadcast_to([P, H, SEQ - 1]),
                                         ALU.mult).then_inc(dist_done, 1)
                        pool.wait_ge(dist_done, u + 1)
                        pool.wait_ge(cc_ready, u + 1)
                        g_.tensor_tensor(wd[:, :, 0:SEQ - 1], wd[:, :, 0:SEQ - 1],
                                         cc[:, slot, :, None].broadcast_to([P, H, SEQ - 1]),
                                         ALU.mult).then_inc(scaled_done, 1)
                    elif kind == "SUB2":
                        p = stage[2]
                        u, slot = pair_no(2, p, i), pair_slot(2, p, 2)
                        t = PAIR_TAILS.number(seg, i, ("T", 2, p))
                        pool.wait_ge(shifted_t, count(2 * t - 2))
                        pool.wait_ge(max2_ready, u + 1)
                        g_.tensor_tensor(ss[:, PAIR_TAILS.slot(seg, i, ("T", 2, p), 2), :, :, :]
                                         .rearrange("p h g k -> p g h k"),
                                         te[:, slot, :, :].rearrange("p (g h) k -> p g h k", g=2),
                                         mx2[:, slot, :, :, None].broadcast_to([P, 2, HH, SEQ]),
                                         ALU.subtract).then_inc(sub2_done, 1)
                    elif kind == "XLB":
                        pool.wait_ge(*left(seg, i, ("Y0",)))
                        if seg == 1:
                            b, n = misc(seg, i, ("OP", 2))
                            pool.wait_ge(misc_ready[b], n + 1)
                        g_.tensor_tensor(xLb[:, :], xL[:, :], vec("bo2").broadcast_to([P, TOK]), ALU.add).then_inc(xlb_done, 1)
                    elif kind == "OUT":
                        pool.wait_ge(stored, 16 * i)
                        b, n = misc(seg, i, ("Y1",))
                        pool.wait_ge(misc_left[b], n + 1)
                        g_.tensor_tensor(yo[:, :, :], xn[:, 1, :, :],
                                         ln2[:, 0:1, :].broadcast_to([P, PAIRS, D]), ALU.mult).then_inc(gain_done, 1)
                        pool.wait_ge(gain_done, i)
                        g_.tensor_tensor(yo[:, :, :], yo[:, :, :],
                                         ln2[:, 1:2, :].broadcast_to([P, PAIRS, D]), ALU.add).then_inc(y_ready, 1)

            run(pool, body)


def kernel(**inputs):
    import numpy as np
    import concourse.bacc as bacc
    from concourse.bass_utils import run_bass_kernel_spmd

    a = {n: np.asarray(v) for n, v in inputs.items()}
    f32 = np.float32

    def blocks(m):
        return m.reshape(CHUNKS, P, D).transpose(1, 0, 2).reshape(P, CHUNKS * D)

    l0, l1 = "L0_xattn_", "L1_xattn_"
    mats = {"q0": a[l0 + "sWq"], "k0": a[l0 + "sWk"], "v0": a[l0 + "sWv"], "o0": a[l0 + "sWo"],
            "q1": a[l0 + "cWq"], "k1": a[l0 + "cWk"], "v1": a[l0 + "cWv"], "o1": a[l0 + "cWo"],
            "w1_0": a[l0 + "W1"], "w2_0": blocks(a[l0 + "W2"]),
            "q2": a[l1 + "Wk"].T, "v2": a[l1 + "Wv"].T, "o2": a[l1 + "Wo"].T,
            "w1_1": a[l1 + "W1"].T, "w2_1": blocks(a[l1 + "W2"].T)}
    weights = np.concatenate([mats[n] for n in W_COLS], axis=1)
    small = {"bq0": "sbq", "bk0": "sbk", "bv0": "sbv", "bo0": "sbo", "bq1": "cbq", "bk1": "cbk", "bv1": "cbv",
             "bo1": "cbo", "b2_0": "b2"}
    small = {n: a[l0 + m] for n, m in small.items()}
    small.update({"bk2": a[l1 + "bk"], "bv2": a[l1 + "bv"], "bo2": a[l1 + "bo"], "ln1_w": a[l1 + "ln1_w"],
                  "ln1_b": a[l1 + "ln1_b"], "b2_1": a[l1 + "b2"]})
    for c in range(CHUNKS):
        small[f"b1_0_{c}"] = a[l0 + "b1"][c * P:(c + 1) * P]
        small[f"b1_1_{c}"] = a[l1 + "b1"][c * P:(c + 1) * P]
    vecs = np.stack([small[n] for n in VECS], axis=1)
    rows = np.broadcast_to(np.stack([a[l1 + "ln2_w"], a[l1 + "ln2_b"]]), (P, 2, D))
    gam = np.broadcast_to(a[l1 + "gammas"].reshape(1, H), (P, H))

    consts = np.zeros((P, C_TOTAL), f32)
    part = np.arange(P)
    consts[:, C_IDENT:C_IDENT + P] = np.eye(P)
    consts[:, C_HEAD:C_HEAD + HH] = (part[:, None] // DK) % HH == np.arange(HH)
    ahead = (part % SEQ)[:, None] - np.arange(SEQ)[None, :]
    consts[:, C_CAUSAL:C_CAUSAL + SEQ] = np.where(ahead >= 0, 0.0, NEG1)
    consts[:, C_DIST:C_DIST + SEQ] = np.maximum(ahead, 0)
    consts[:, C_CARRY:C_CARRY + H * SEQ] = np.tile(np.arange(SEQ) < SEQ - 1, H)
    ones = np.zeros((P, HH, VW), f32)
    ones[:P // 2, :, DK] = 1
    ones[P // 2:, :, 2 * DK + 1] = 1
    consts[:, C_VONE:] = ones.reshape(P, HH * VW)

    arrays = {"x": a["x"].reshape(-1, D), "ctx_in": a["ctx_1024"].reshape(-1, D),
              "mask0": a["mask_Bx1xSxS2_bk0"].reshape(-1, SEQ),
              "mask1": a["mask_Bx1xSxS2_bf1"].reshape(-1, SEQ),
              "weights": weights, "vecs": vecs, "rows": rows, "gam": gam, "consts": consts}
    arrays = {n: np.ascontiguousarray(v) for n, v in arrays.items()}
    nc = bacc.Bacc("TRN2", target_bir_lowering=False, num_devices=1)
    args = [nc.dram_tensor(n, v.shape, mybir.dt.from_np(v.dtype), kind="ExternalInput").ap()
            for n, v in arrays.items()]
    args.append(nc.dram_tensor("out", (NB * SEQ, D), mybir.dt.float32, kind="ExternalOutput").ap())
    build(nc, *args)
    r = run_bass_kernel_spmd(nc, [arrays], core_ids=[0])
    return r.results[0]["out"].reshape(NB, SEQ, D)
```

```python
import concourse.bass as bass
from concourse import mybir
from contextlib import ExitStack

P = 128
NB, SEQ, D, H, DK, DFF = 128, 64, 128, 16, 8, 512
PAIRS = 4
TOK = PAIRS * P
GROUPS = NB * SEQ // TOK
HH = H // 2
HALF = HH * SEQ
CHUNKS = DFF // P
VW = 2 * (DK + 1)
W_COLS = {}
_at = 0
for _n, _w in (("q0", D), ("k0", D), ("v0", D), ("o0", D), ("q1", D), ("k1", D), ("v1", D), ("o1", D),
               ("w1_0", DFF), ("w2_0", DFF), ("q2", D), ("v2", D), ("o2", D), ("w1_1", DFF), ("w2_1", DFF)):
    W_COLS[_n] = (_at, _at + _w)
    _at += _w
W_TOTAL = _at
VECS = ["bq0", "bk0", "bv0", "bo0", "bq1", "bk1", "bv1", "bo1", "b2_0", "bk2", "bv2", "bo2", "ln1_w", "ln1_b",
        "b2_1", "b1_0_0", "b1_0_1", "b1_0_2", "b1_0_3", "b1_1_0", "b1_1_1", "b1_1_2", "b1_1_3"]
C_IDENT, C_HEAD, C_CAUSAL, C_DIST, C_CARRY, C_VONE = 0, 128, 136, 200, 264, 1288
C_TOTAL = C_VONE + HH * VW
NEG0, NEG1, EPS = -1.0e9, -1.0e32, 1.0e-5
TINY = 1.0e-18
SCALE = float(DK) ** -0.5

ORDERS = (
    """
MASK.0 XT get.XT K.0 get.K.0 KM.0 Q.0 get.Q.0 S.0.0 D1.0.0 SUB.0.0 S.0.1 D1.0.1 S.0.2 D1.0.2 T.0.0 PX.0.0 V.0
SUB.0.1 get.V.0 S.0.3 SUB.0.2 T.0.1 PX.0.1 D1.0.3 PV.0.0 SUB.0.3 T.0.2 N.0.0 PX.0.2 PV.0.1 N.0.1 T.0.3 PX.0.3
PV.0.2 N.0.2 PV.0.3 N.0.3
""",
    """
CT get.CT MASK.0 OT.0 get.OT.0 K.1 get.K.1 OP.0 get.OP.0 XT MASK.1 get.XT K.0 Q.0 get.K.0 KM.0 get.Q.0 S.0.0
KM.1 Q.1 get.Q.1 D1.0.0 V.0 S.1.0 D1.1.0 V.1 S.1.1 SUB.0.0 get.V.0 T.0.0 D1.1.1 S.0.1 PX.0.0 SUB.1.0 T.1.0
PV.0.0 D1.0.1 K.2 get.V.1 SUB.1.1 N.0.0 get.K.2 S.0.2 D1.0.2 PX.1.0 PV.1.0 N.1.0 SUB.0.1 T.0.1 S.1.2 D1.1.2
SUB.0.2 PX.0.1 T.1.1 PV.0.1 PX.1.1 N.0.1 S.0.3 T.0.2 D1.0.3 PX.0.2 SUB.1.2 PV.1.1 S.1.3 SUB.0.3 T.1.2 N.1.1
D1.1.3 PV.0.2 PX.1.2 SUB.1.3 N.0.2 T.0.3 PX.0.3 PV.1.2 T.1.3 PX.1.3 N.1.2 PV.0.3 V.2 N.0.3 PV.1.3 get.V.2 N.1.3
""",
    """
CT OT.1 get.CT OT.0 get.OT.1 OP.1 get.OP.1 get.OT.0 OP.0 H.0.1 MASK.0 get.H.0.1 get.OP.0 H.0.3 MASK.1 get.H.0.3
H.0.2 get.H.0.2 H.0.0 K.1 get.H.0.0 Y0 get.K.1 XT get.Y0 XLB KM.1 get.XT Q.2 K.0 get.Q.2 get.K.0 KM.2 S.2.0
D1.2.0 Q.0 S.2.1 V.0 KM.0 SUB.2.0 get.Q.0 D1.2.1 E1.2.0 D2.2.0 get.V.0 PM.2.0 S.0.0 Q.1 D1.0.0 get.Q.1 SUB.2.1
LG.2.0 E1.2.1 S.1.0 SUB.0.0 D1.1.0 D2.2.1 S.2.2 D3.2.0 T.0.0 SUB.1.0 PM.2.1 PX.0.0 D1.2.2 SUB.2.2 V.1 S.0.1
T.1.0 PV.0.0 get.V.1 D1.0.1 PX.1.0 SUB2.2.0 S.1.1 E1.2.2 N.0.0 D2.2.2 T.2.0 D1.1.1 S.2.3 PV.1.0 SUB.0.1 LG.2.1
K.2 PX.2.0 D3.2.1 N.1.0 PM.2.2 T.0.1 SUB.1.1 PV.2.0 D1.2.3 SUB2.2.1 PX.0.1 N.2.0 S.0.2 D1.0.2 LG.2.2 T.1.1
SUB.2.3 PV.0.1 E1.2.3 N.0.1 S.1.2 PX.1.1 T.2.1 PX.2.1 D1.1.2 PV.1.1 N.1.1 SUB.0.2 D2.2.3 D3.2.2 T.0.2 SUB.1.2
PV.2.1 S.0.3 N.2.1 PX.0.2 T.1.2 PV.0.2 PM.2.3 PX.1.2 D1.0.3 SUB2.2.2 N.0.2 S.1.3 SUB.0.3 LG.2.3 D1.1.3 PV.1.2
T.2.2 PX.2.2 SUB.1.3 T.0.3 D3.2.3 N.1.2 PV.2.2 PX.0.3 T.1.3 N.2.2 PX.1.3 PV.0.3 SUB2.2.3 N.0.3 T.2.3 PX.2.3
get.K.2 PV.1.3 N.1.3 PV.2.3 N.2.3 V.2 get.V.2
""",
    """
OT.1 KM.2 CT get.OT.1 OT.0 get.CT get.OT.0 OP.1 K.1 get.K.1 get.OP.1 H.0.0 H.0.1 MASK.0 get.H.0.0 H.0.3
get.H.0.1 H.0.2 get.H.0.3 get.H.0.2 Y0 get.Y0 KM.1 OP.0 XT get.OP.0 get.XT Q.2 get.Q.2 K.0 S.2.0 get.K.0 D1.2.0
SUB.2.0 KM.0 Q.0 get.Q.0 S.2.1 E1.2.0 V.0 D1.2.1 get.V.0 S.0.0 D2.2.0 Q.1 PM.2.0 get.Q.1 OT.2 MASK.1 get.OT.2
D1.0.0 SUB.2.1 S.1.0 SUB.0.0 LG.2.0 D1.1.0 OP.2 E1.2.1 LN.0.0 D3.2.0 S.2.2 SUB.1.0 V.1 T.0.0 LN.0.1 PX.0.0
SUB2.2.0 PV.0.0 NX.0 T.1.0 PX.1.0 D2.2.1 X2T N.0.0 T.2.0 XLB D1.2.2 S.0.1 get.V.1 PM.2.1 D1.0.1 get.X2T PV.1.0
PX.2.0 H.1.3 S.1.1 SUB.2.2 get.H.1.3 E1.2.2 SUB.0.1 N.1.0 LG.2.1 D1.1.1 S.0.2 PV.2.0 D2.2.2 T.0.1 D1.0.2 SUB.1.1
H.1.0 H.1.1 get.H.1.0 PX.0.1 N.2.0 PM.2.2 S.2.3 T.1.1 D3.2.1 get.H.1.1 H.1.2 SUB2.2.1 D1.2.3 S.1.2 PV.0.1 D1.1.2
LG.2.2 PX.1.1 T.2.1 SUB.2.3 SUB.0.2 PX.2.1 N.0.1 S.0.3 PV.1.1 T.0.2 E1.2.3 SUB.1.2 D2.2.3 N.1.1 PX.0.2 D1.0.3
PV.2.1 T.1.2 PM.2.3 get.H.1.2 LG.2.3 N.2.1 S.1.3 D3.2.2 SUB.0.3 PV.0.2 SUB2.2.2 Y1 D1.1.3 PX.1.2 N.0.2 T.2.2
PV.1.2 PX.2.2 D3.2.3 T.0.3 N.1.2 SUB.1.3 LN.1.0 PV.2.2 PX.0.3 T.1.3 SUB2.2.3 PX.1.3 N.2.2 PV.0.3 K.2 N.0.3
PV.1.3 T.2.3 N.1.3 LN.1.1 PX.2.3 NX.1 PV.2.3 get.K.2 V.2 N.2.3 OUT get.V.2
""",
    """
OT.1 CT get.OT.1 OP.1 get.CT OT.0 get.OP.1 H.0.1 get.OT.0 get.H.0.1 H.0.0 H.0.3 KM.2 get.H.0.0 get.H.0.3 H.0.2
get.H.0.2 Y0 K.1 get.Y0 get.K.1 Q.2 get.Q.2 OP.0 get.OP.0 S.2.0 D1.2.0 S.2.1 D1.2.1 MASK.1 KM.1 SUB.2.0 E1.2.0
Q.1 OT.2 get.Q.1 S.1.0 get.OT.2 D2.2.0 PM.2.0 SUB.2.1 D1.1.0 OP.2 SUB.1.0 V.1 LG.2.0 E1.2.1 get.V.1 D2.2.1
LN.0.0 PM.2.1 S.2.2 D3.2.0 T.1.0 SUB2.2.0 PX.1.0 D1.2.2 SUB.2.2 LN.0.1 PV.1.0 S.1.1 NX.0 D1.1.1 LG.2.1 T.2.0
E1.2.2 X2T get.X2T PX.2.0 D2.2.2 S.2.3 N.1.0 SUB.1.1 H.1.1 H.1.3 D3.2.1 get.H.1.1 D1.2.3 PM.2.2 PV.2.0 N.2.0
T.1.1 get.H.1.3 PX.1.1 S.1.2 LG.2.2 H.1.2 PV.1.1 SUB2.2.1 D1.1.2 SUB.2.3 T.2.1 E1.2.3 D2.2.3 S.1.3 PX.2.1
get.H.1.2 SUB.1.2 H.1.0 get.H.1.0 N.1.1 T.1.2 D3.2.2 PM.2.3 PV.2.1 Y1 PX.1.2 LG.2.3 N.2.1 PV.1.2 SUB2.2.2 T.2.2
D1.1.3 PX.2.2 SUB.1.3 LN.1.0 T.1.3 N.1.2 PV.2.2 K.2 LN.1.1 D3.2.3 N.2.2 PX.1.3 SUB2.2.3 PV.1.3 T.2.3 NX.1 PX.2.3
N.1.3 PV.2.3 V.2 N.2.3 get.K.2 OUT XLB get.V.2
""",
    """
KM.2 OT.1 OT.2 get.OT.1 OP.1 get.OP.1 get.OT.2 H.0.2 H.0.3 get.H.0.2 H.0.0 get.H.0.3 H.0.1 get.H.0.0 get.H.0.1
Y0 get.Y0 Q.2 get.Q.2 S.2.0 D1.2.0 SUB.2.0 E1.2.0 D2.2.0 OP.2 LN.0.0 S.2.1 PM.2.0 D1.2.1 LN.0.1 SUB.2.1 NX.0 X2T
E1.2.1 D2.2.1 LG.2.0 PM.2.1 get.X2T S.2.2 LG.2.1 D3.2.0 D1.2.2 H.1.1 D3.2.1 H.1.3 SUB2.2.0 T.2.0 SUB.2.2 PX.2.0
S.2.3 get.H.1.1 E1.2.2 XLB D2.2.2 D1.2.3 PM.2.2 SUB.2.3 get.H.1.3 SUB2.2.1 E1.2.3 LG.2.2 D2.2.3 H.1.2 PV.2.0
N.2.0 T.2.1 H.1.0 PX.2.1 PM.2.3 PV.2.1 D3.2.2 N.2.1 get.H.1.0 get.H.1.2 Y1 LG.2.3 SUB2.2.2 D3.2.3 T.2.2 SUB2.2.3
PX.2.2 LN.1.0 PV.2.2 LN.1.1 N.2.2 T.2.3 NX.1 PX.2.3 PV.2.3 OUT N.2.3
""",
    """
OT.2 get.OT.2 OP.2 LN.0.0 LN.0.1 NX.0 X2T get.X2T H.1.2 H.1.1 get.H.1.2 H.1.3 get.H.1.1 get.H.1.3 H.1.0
get.H.1.0 Y1 LN.1.0 LN.1.1 NX.1 OUT
""",
)
AGES = {"XT": 0, "CT": 1, "K": (0, 1, 1), "V": (0, 1, 1), "Q": (0, 1, 2), "KM": (0, 1, 2), "MASK": (0, 1),
        "OT": (1, 2, 3), "OP": (1, 2, 3), "H": (2, 3), "Y0": 2, "XLB": 2, "X2T": 3, "Y1": 3, "LN": (3, 3),
        "NX": (3, 3), "OUT": 3}
AGES.update({n: (0, 1, 2) for n in ("S", "D1", "SUB", "E1", "D2", "PM", "LG", "D3", "SUB2", "T", "PX", "PV", "N")})
LAST_AGE = 3
KM_ON_ACT = (0, 1)


def parse(word):
    return tuple(int(n) if n.isdigit() else n for n in word.split("."))


def age(stage):
    name, *operands = stage[1:] if stage[0] == "get" else stage
    return AGES[name][operands[0]] if operands else AGES[name]


MISC_USES = {"XT", "CT", "K", "Q", "V", "OT", "OP", "X2T", "H", "Y0", "Y1"}
LOOP = LAST_AGE
SEGMENTS = [[parse(word) for word in order.split()] for order in ORDERS]
LENGTHS = [1, 1, 1, GROUPS - LAST_AGE, 1, 1, 1]


class Turns:

    def __init__(self, kinds, attentions=(0, 1, 2)):
        self.lists = [[s for s in seg if s[0] in kinds and (len(s) < 3 or s[0] == "H" or s[1] in attentions)]
                      for seg in SEGMENTS]

    def at(self, seg, i, stage):
        c = sum(LENGTHS[k] * len(self.lists[k]) for k in range(seg)) + self.lists[seg].index(stage)
        return (c, len(self.lists[seg]), i - LOOP) if seg == LOOP else (c, 0, 0)

    def number(self, seg, i, stage):
        c, n, j = self.at(seg, i, stage)
        return c + j * n if n else c

    def before(self, seg, i):
        c = sum(LENGTHS[k] * len(self.lists[k]) for k in range(seg))
        return c + (i - LOOP) * len(self.lists[seg]) if seg == LOOP else c

    def slot(self, seg, i, stage, slots):
        c, n, _ = self.at(seg, i, stage)
        assert n % slots == 0
        return c % slots

    def turn_of_slot(self, seg, i, stage, slots):
        c, n, j = self.at(seg, i, stage)
        return c // slots + j * (n // slots) if n else c // slots


PAIR_SCORES = Turns({"S"})
LAYER0_SCORES = Turns({"S"}, (0, 1))
PAIR_TAILS = Turns({"T"})
MISC = Turns(MISC_USES)


def count(value):
    return max(value, 0) if isinstance(value, int) else value


def build(nc, x, ctx_in, mask0, mask1, weights, vecs, rows, gam, consts, out):
    F32, U8 = mybir.dt.float32, mybir.dt.uint8
    ALU, ACT, AX = mybir.AluOpType, mybir.ActivationFunctionType, mybir.AxisListType

    with ExitStack() as ctx:
        def sb(name, shape, dt=F32):
            return ctx.enter_context(nc.sbuf_tensor(name, [P] + shape, dt))

        def sem(name):
            return ctx.enter_context(nc.semaphore(name))

        def sems(name, n):
            return [sem(f"{name}{k}") for k in range(n)]

        W = sb("W", [W_TOTAL])
        V = sb("V", [len(VECS)])
        ln2 = sb("ln2", [2, D])
        const = sb("const", [C_TOTAL])
        gamma2 = sb("gamma2", [H])
        gtmp = sb("gtmp", [4, H])
        bqs = sb("bqs", [3])
        bln = sb("bln", [1])
        epsc = sb("epsc", [2])
        ident = const[:, C_IDENT:C_IDENT + P]
        head_rows = const[:, C_HEAD:C_HEAD + HH]
        causal = const[:, C_CAUSAL:C_CAUSAL + SEQ]
        distance = const[:, C_DIST:C_DIST + SEQ]
        carry = const[:, C_CARRY:C_CARRY + 2 * HALF]
        vone = const[:, C_VONE:C_VONE + HH * VW]

        def w(name):
            return W[:, W_COLS[name][0]:W_COLS[name][1]]

        def vec(name):
            k = VECS.index(name)
            return V[:, k:k + 1]

        xin = sb("xin", [PAIRS, D])
        cin = sb("cin", [PAIRS, D])
        min_ = [sb(f"mask_in{f}", [PAIRS, SEQ], U8) for f in range(2)]
        bias = [sb(f"mask_bias{f}", [PAIRS, SEQ]) for f in range(2)]
        some = [sb(f"some_key{f}", [PAIRS]) for f in range(2)]
        xA, xB, xF, xL, xLb, cT = (sb(n, [TOK]) for n in ("xA", "xB", "xF", "xL", "xLb", "cT"))
        x2T, x2bT = sb("x2T", [TOK]), sb("x2bT", [TOK])
        qT = [sb(f"qT{f}", [TOK]) for f in range(3)]
        kT = [sb(f"kT{f}", [TOK]) for f in range(3)]
        vb = [sb(f"vb{f}", [2 * PAIRS, HH, VW]) for f in range(3)]
        oT = [sb(f"oT{f}", [TOK]) for f in range(3)]
        hT = [sb(f"hT{l}", [CHUNKS, TOK]) for l in range(2)]
        on = [sb(f"on{f}", [PAIRS, D]) for f in range(3)]
        xn = sb("xn", [2, PAIRS, D])
        yo = sb("yo", [PAIRS, D])
        st6 = sb("st6", [2, PAIRS, 6])
        mv = sb("mv", [2, PAIRS, 2])
        rstd = sb("rstd", [2, PAIRS])
        lnv = sb("lnv", [2, PAIRS])
        km = [sb(f"km{f}", [HH, TOK]) for f in range(3)]
        sm = [sb("sm0", [2, 2, HALF]), sb("sm1", [2, 2, HALF])]
        mx = [sb("mx0", [2, 2, HH]), sb("mx1", [2, 2, HH])]
        mx2 = sb("mx2", [2, 2, HH])
        ss = sb("ss", [2, HH, 2, SEQ])
        pt = sb("pt", [2, HH, P])
        ex = sb("ex", [H, SEQ])
        suf = sb("suf", [H, SEQ])
        wd = sb("wd", [H, SEQ])
        te = sb("te", [2, H, SEQ])
        rtot = sb("rtot", [2, H])
        cc = sb("cc", [2, H])
        rz = sb("rz", [2, H])

        s_ps = [ctx.enter_context(nc.psum_tensor(f"s_ps{n}", [P, 512], F32)) for n in range(3)]
        t_ps = [ctx.enter_context(nc.psum_tensor(f"t_ps{n}", [P, 512], F32)) for n in range(2)]
        o_ps = ctx.enter_context(nc.psum_tensor("o_ps", [P, 512], F32))
        m_ps = [ctx.enter_context(nc.psum_tensor(f"m_ps{n}", [P, 512], F32)) for n in range(2)]

        const_loaded = sem("const_loaded")
        x_loaded, c_loaded, mask_loaded = sem("x_loaded"), sem("c_loaded"), sems("mask_loaded", 2)
        setup_act, setup_dve, setup_pool = sem("setup_act"), sem("setup_dve"), sem("setup_pool")
        misc_ready = sems("misc_ready", 2)
        misc_left = sems("misc_left", 2)
        bias_done = sems("bias_done", 2)
        km_ready = sems("km_ready", 3)
        scores_ready = sem("scores_ready")
        scores_left = sem("scores_left")
        max_ready = sems("max_ready", 2)
        sub_done = sems("sub_done", 2)
        exp1_done, scan_done, cc_ready = sem("exp1_done"), sem("scan_done"), sem("cc_ready")
        rtot_done = sem("rtot_done")
        dist_done, scaled_done = sem("dist_done"), sem("scaled_done")
        ln_done, root_done, effect_ready = sem("ln_done"), sem("root_done"), sem("effect_ready")
        s2_done, max2_ready, sub2_done = sem("s2_done"), sem("max2_ready"), sem("sub2_done")
        shifted_t = sem("shifted_t")
        probs_ready = sem("probs_ready")
        pv_done = sem("pv_done")
        rz_done, norm_done = sem("rz_done"), sem("norm_done")
        xlb_done = sem("xlb_done")
        stats_done, mean_ready = sem("stats_done"), sem("mean_ready")
        lnv_done, rstd_ready = sem("lnv_done"), sem("rstd_ready")
        gain_done, y_ready, stored = sem("gain_done"), sem("y_ready"), sem("stored")

        xv = x.rearrange("(n p) d -> p n d", p=P)
        cv = ctx_in.rearrange("(n p) d -> p n d", p=P)
        mv0 = mask0.rearrange("(n p) k -> p n k", p=P)
        mv1 = mask1.rearrange("(n p) k -> p n k", p=P)
        ov = out.rearrange("(n p) d -> p n d", p=P)

        def layer(f):
            return 1 if f == 2 else 0

        def score_turn(seg, i, f, p):
            if f == 2:
                return (i - 2) * PAIRS + p, p % 2
            return (LAYER0_SCORES.number(seg, i, ("S", f, p)), LAYER0_SCORES.slot(seg, i, ("S", f, p), 2))

        def run(eng, body):
            for i in range(LOOP):
                body(i, i)
            with eng.Fori(LOOP, GROUPS) as i:
                body(LOOP, i)
            for k in range(LAST_AGE):
                body(LOOP + 1 + k, GROUPS + k)

        def misc(seg, i, stage):
            return MISC.slot(seg, i, stage, 2), MISC.turn_of_slot(seg, i, stage, 2)

        def all_left(seg, i, b):
            uses = MISC.before(seg, i)
            if seg != LOOP:
                return (uses + 1 - b) // 2
            return (MISC.before(seg, LOOP) + 1 - b) // 2 + (i - LOOP) * (len(MISC.lists[seg]) // 2)

        def left(seg, i, stage):
            b, n = misc(seg, i, stage)
            return misc_left[b], n + 1

        block = ctx.enter_context(nc.Block())

        @block.sync
        def _(sp):
            sp.dma_start(const[:, :], consts).then_inc(const_loaded, 16)
            sp.dma_start(W[:, :], weights).then_inc(const_loaded, 16)
            sp.dma_start(V[:, :], vecs).then_inc(const_loaded, 16)
            sp.dma_start(gtmp[:, 0, :], gam).then_inc(const_loaded, 16)
            sp.dma_start(ln2[:, :, :], rows).then_inc(stored, 16)

            def load_x(g):
                sp.dma_start(xin[:, :, :], xv[:, bass.ds(g * PAIRS, PAIRS), :]).then_inc(x_loaded, 16)
                sp.dma_start(min_[0][:, :, :], mv0[:, bass.ds(g * PAIRS, PAIRS), :]).then_inc(mask_loaded[0], 16)

            def load_c(g):
                sp.dma_start(cin[:, :, :], cv[:, bass.ds(g * PAIRS, PAIRS), :]).then_inc(c_loaded, 16)
                sp.dma_start(min_[1][:, :, :], mv1[:, bass.ds(g * PAIRS, PAIRS), :]).then_inc(mask_loaded[1], 16)

            def next_x(seg, i):
                b, n = misc(seg, i, ("XT",))
                sp.wait_ge(misc_ready[b], n + 1)
                sp.nop(nofuse=True)
                sp.wait_ge(bias_done[0], 2 * (i + 1))
                sp.nop(nofuse=True)
                load_x(i + 1)

            def next_c(seg, i):
                b, n = misc(seg, i, ("CT",))
                sp.wait_ge(misc_ready[b], n + 1)
                sp.nop(nofuse=True)
                sp.wait_ge(bias_done[1], 2 * i)
                sp.nop(nofuse=True)
                load_c(i)

            def store(i):
                sp.wait_ge(y_ready, i - 1)
                sp.nop(nofuse=True)
                sp.dma_start(ov[:, bass.ds((i - 3) * PAIRS, PAIRS), :], yo[:, :, :]).then_inc(stored, 16)

            load_x(0)
            load_c(0)
            next_x(0, 0)
            for i in range(1, LOOP):
                next_x(i, i)
                next_c(i, i)
            with sp.Fori(LOOP, GROUPS - 1) as i:
                next_x(LOOP, i)
                next_c(LOOP, i)
                store(i)
            next_c(LOOP, GROUPS - 1)
            for i in range(GROUPS - 1, GROUPS + LAST_AGE):
                store(i)
            sp.wait_ge(stored, 16 * (GROUPS + 1))

        @block.tensor
        def _(pe):
            mm, tr = nc.tensor.matmul, nc.tensor.transpose
            pe.wait_ge(const_loaded, 64)

            def take(seg, i, stage):
                b, n = misc(seg, i, stage)
                pe.wait_ge(misc_left[b], n)
                pe.nop(nofuse=True)
                return b

            def body(seg, i):
                for stage in SEGMENTS[seg]:
                    kind = stage[0]
                    if kind in ("XT", "CT"):
                        b = take(seg, i, stage)
                        pe.wait_ge(x_loaded if kind == "XT" else c_loaded, 16 * (i + 1 - age(stage)))
                        src = xin if kind == "XT" else cin
                        for j in range(PAIRS):
                            last = tr(m_ps[b][:, j * P:(j + 1) * P], src[:, j, :], ident)
                        last.then_inc(misc_ready[b], 1)
                    elif kind in ("Q", "K"):
                        f = stage[1]
                        b = take(seg, i, stage)
                        if f == 0:
                            pe.wait_ge(*left(seg, i, ("XT",)))
                        elif kind == "K":
                            pe.wait_ge(*left(seg, i, ("CT",)))
                        elif kind == "Q" and f == 1:
                            pe.wait_ge(*left(seg, i, ("OP", 0)))
                        elif kind == "Q" and f == 2:
                            pe.wait_ge(*left(seg, i, ("Y0",)))
                        src = {("Q", 0): xA, ("K", 0): xA, ("Q", 1): xB, ("K", 1): cT, ("Q", 2): xL,
                               ("K", 2): cT}[kind, f]
                        wt = w("q2") if f == 2 else w(f"{kind.lower()}{f}")
                        mm(m_ps[b][:, :], wt, src[:, :], start=True, stop=True).then_inc(misc_ready[b], 1)
                    elif kind == "V":
                        f = stage[1]
                        b = take(seg, i, stage)
                        pe.wait_ge(*left(seg, i, ("XT",) if f == 0 else ("CT",)))
                        src = xA if f == 0 else cT
                        wv = w(f"v{f}")
                        for n in range(2 * PAIRS):
                            for g in range(2):
                                last = mm(m_ps[b][64 * g:64 * g + 64, n * 64:(n + 1) * 64],
                                          src[:, n * SEQ:(n + 1) * SEQ], wv[:, 64 * g:64 * g + 64],
                                          start=True, stop=True)
                        last.then_inc(misc_ready[b], 1)
                    elif kind == "S":
                        _, f, p = stage
                        n = PAIR_SCORES.number(seg, i, stage)
                        if p == 0:
                            pe.wait_ge(*left(seg, i, ("Q", f)))
                            pe.wait_ge(km_ready[f], i - f + 1)
                        c, per, _ = PAIR_SCORES.at(seg, i, stage)
                        for g in range(2):
                            bank = (2 * c + g) % 3
                            assert (2 * per) % 3 == 0
                            pe.wait_ge(scores_left, count(2 * n + g - 2))
                            pe.nop(nofuse=True)
                            pe.nop(nofuse=True)
                            for s in range(2):
                                t0 = (2 * p + s) * SEQ
                                last = mm(s_ps[bank][64 * s:64 * s + 64, :], qT[f][64 * g:64 * g + 64, t0:t0 + SEQ],
                                          km[f][64 * g:64 * g + 64, :, t0:t0 + SEQ],
                                          start=True, stop=True)
                            last.then_inc(scores_ready, 1)
                    elif kind == "T":
                        _, f, p = stage
                        u, _ = score_turn(seg, i, f, p)
                        t = PAIR_TAILS.number(seg, i, stage)
                        slot = PAIR_TAILS.slot(seg, i, stage, 2)
                        if f == 2:
                            pe.wait_ge(sub2_done, u + 1)
                        else:
                            pe.wait_ge(sub_done[0], 2 * u + 2)
                        for q in range(2):
                            pe.wait_ge(probs_ready, count(2 * t - 1 + q))
                            for j in range(4):
                                last = tr(t_ps[q][:, j * P:(j + 1) * P], ss[:, slot, 4 * q + j, :, :], ident)
                            last.then_inc(shifted_t, 1)
                    elif kind == "PV":
                        _, f, p = stage
                        t = PAIR_TAILS.number(seg, i, ("T", f, p))
                        slot = PAIR_TAILS.slot(seg, i, ("T", f, p), 2)
                        if p == 0 and f < 2:
                            pe.wait_ge(*left(seg, i, ("V", f)))
                        elif p == 0:
                            pe.wait_ge(misc_left[0], all_left(seg, i, 0))
                            pe.wait_ge(misc_left[1], all_left(seg, i, 1))
                        pe.wait_ge(norm_done, t)
                        for q in range(2):
                            pe.wait_ge(probs_ready, 2 * t + 1 + q)
                            for hh in range(4 * q, 4 * q + 4):
                                for s in range(2):
                                    last = mm(o_ps[64 * s:64 * s + 64, hh * VW:(hh + 1) * VW],
                                              pt[:, slot, hh, 64 * s:64 * s + 64], vb[f][:, 2 * p + s, hh, :],
                                              start=True, stop=True)
                        last.then_inc(pv_done, 1)
                    elif kind == "OT":
                        f = stage[1]
                        b = take(seg, i, stage)
                        pe.wait_ge(norm_done, PAIR_TAILS.before(seg, i))
                        for j in range(PAIRS):
                            last = tr(m_ps[b][:, j * P:(j + 1) * P], on[f][:, j, :], ident)
                        last.then_inc(misc_ready[b], 1)
                    elif kind == "OP":
                        f = stage[1]
                        b = take(seg, i, stage)
                        pe.wait_ge(*left(seg, i, ("OT", f)))
                        if f < 2:
                            last = mm(m_ps[b][:, :], w(f"o{f}"), oT[f][:, :], start=True, stop=True)
                        else:
                            pe.wait_ge(xlb_done, i - 2)
                            for j in range(PAIRS):
                                o = m_ps[b][:, j * P:(j + 1) * P]
                                mm(o, xLb[:, j * P:(j + 1) * P], ident, start=True, stop=False)
                                last = mm(o, oT[f][:, j * P:(j + 1) * P], w("o2"), start=False, stop=True)
                        last.then_inc(misc_ready[b], 1)
                    elif kind == "X2T":
                        b = take(seg, i, stage)
                        pe.wait_ge(*left(seg, i, ("OP", 2)))
                        for j in range(PAIRS):
                            last = tr(m_ps[b][:, j * P:(j + 1) * P], xn[:, 0, j, :], ident)
                        last.then_inc(misc_ready[b], 1)
                    elif kind == "H":
                        _, l, c = stage
                        b = take(seg, i, stage)
                        pe.wait_ge(*left(seg, i, ("X2T",) if l else ("OP", 1)))
                        mm(m_ps[b][:, :], w(f"w1_{l}")[:, c * P:(c + 1) * P], (x2T if l else xF)[:, :],
                           start=True, stop=True).then_inc(misc_ready[b], 1)
                    elif kind == "Y0":
                        b = take(seg, i, stage)
                        for c in range(CHUNKS):
                            pe.wait_ge(*left(seg, i, ("H", 0, c)))
                            last = mm(m_ps[b][:, :], w("w2_0")[:, c * P:(c + 1) * P], hT[0][:, c, :],
                                      start=c == 0, stop=c == CHUNKS - 1)
                        last.then_inc(misc_ready[b], 1)
                    elif kind == "Y1":
                        b = take(seg, i, stage)
                        for c in range(CHUNKS):
                            pe.wait_ge(*left(seg, i, ("H", 1, c)))
                            pe.nop(nofuse=True)
                        for j in range(PAIRS):
                            o = m_ps[b][:, j * P:(j + 1) * P]
                            mm(o, x2bT[:, j * P:(j + 1) * P], ident, start=True, stop=False)
                            for c in range(CHUNKS):
                                last = mm(o, hT[1][:, c, j * P:(j + 1) * P], w("w2_1")[:, c * P:(c + 1) * P],
                                          start=False, stop=c == CHUNKS - 1)
                        last.then_inc(misc_ready[b], 1)

            run(pe, body)

        @block.scalar
        def _(act):
            A = nc.scalar.activation
            nc.scalar.preload_act_table_set("natural_log_exp_and_others")
            act.wait_ge(const_loaded, 64)
            act.wait_ge(setup_dve, 1)
            A(gtmp[:, 2, :], gtmp[:, 1, :], ACT.Exp, scale=-1.0).then_inc(setup_act, 1)
            act.wait_ge(setup_act, 1)
            A(gtmp[:, 3, :], gtmp[:, 2, :], ACT.Ln, bias=1.0).then_inc(setup_act, 1)
            act.wait_ge(setup_dve, 6)

            def evac(seg, i, stage, dst, func, **kw):
                b, n = misc(seg, i, stage)
                act.wait_ge(misc_ready[b], n + 1)
                A(dst, m_ps[b][:, :], func, **kw).then_inc(misc_left[b], 1)

            def body(seg, i):
                for stage in SEGMENTS[seg]:
                    kind = stage[0]
                    if kind == "get":
                        stage = stage[1:]
                        kind = "get " + stage[0]
                    if kind == "KM" and stage[1] in KM_ON_ACT:
                        f = stage[1]
                        if f < 2:
                            act.wait_ge(*left(seg, i, ("K", f)))
                        else:
                            act.wait_ge(misc_left[0], all_left(seg, i, 0))
                            act.wait_ge(misc_left[1], all_left(seg, i, 1))
                        act.wait_ge(scores_ready, 2 * PAIR_SCORES.before(seg, i))
                        for h in range(HH):
                            last = A(km[f][:, h, :], kT[f][:, :], ACT.Copy, scale=head_rows[:, h:h + 1])
                        last.then_inc(km_ready[f], 1)
                    elif kind == "get XT":
                        if seg:
                            act.wait_ge(*left(seg, i, ("OP", 0)))
                        evac(seg, i, stage, xA[:, :], ACT.Copy)
                    elif kind == "get CT":
                        evac(seg, i, stage, cT[:, :], ACT.Copy)
                    elif kind == "get Q":
                        evac(seg, i, stage, qT[stage[1]][:, :], ACT.Identity, bias=bqs[:, stage[1]:stage[1] + 1],
                             scale=SCALE)
                    elif kind == "get K":
                        evac(seg, i, stage, kT[stage[1]][:, :], ACT.Identity, bias=vec(f"bk{stage[1]}"))
                    elif kind == "get V":
                        f = stage[1]
                        b, n = misc(seg, i, stage)
                        act.wait_ge(misc_ready[b], n + 1)
                        if f == 0:
                            act.wait_ge(setup_pool, 3)
                        for g in range(2):
                            last = A(vb[f][64 * g:64 * g + 64, :, :, 9 * g:9 * g + DK],
                                     m_ps[b][64 * g:64 * g + 64, :].rearrange("p (n h d) -> p n h d", h=HH, d=DK),
                                     ACT.Copy)
                        last.then_inc(misc_left[b], 1)
                    elif kind == "E1":
                        u, _ = score_turn(seg, i, 2, stage[2])
                        e = ex[:, :, :]
                        act.wait_ge(sub_done[1], 2 * u + 2)
                        A(e, e, ACT.Exp).then_inc(exp1_done, 1)
                    elif kind == "LG":
                        p = stage[2]
                        u, slot = score_turn(seg, i, 2, p)
                        t = te[:, slot, :, :]
                        act.wait_ge(scaled_done, u + 1)
                        act.wait_ge(sub2_done, count(u - 1))
                        A(t, wd[:, :, :], ACT.Ln, bias=epsc[:, 1:2]).then_inc(ln_done, 1)
                        act.wait_ge(ln_done, u + 1)
                        A(t, t, ACT.Exp, scale=0.5).then_inc(root_done, 1)
                        act.wait_ge(root_done, u + 1)
                        A(t, t, ACT.Exp, scale=-1.0).then_inc(effect_ready, 1)
                    elif kind == "PX":
                        _, f, p = stage
                        t = PAIR_TAILS.number(seg, i, ("T", f, p))
                        slot = PAIR_TAILS.slot(seg, i, ("T", f, p), 2)
                        act.wait_ge(pv_done, count(t - 1))
                        for q in range(2):
                            act.wait_ge(shifted_t, 2 * t + q + 1)
                            A(pt[:, slot, 4 * q:4 * q + 4, :], t_ps[q][:, :].rearrange("p (h t) -> p h t", h=4),
                              ACT.Exp).then_inc(probs_ready, 1)
                    elif kind == "get OT":
                        evac(seg, i, stage, oT[stage[1]][:, :], ACT.Identity, bias=vec(f"bv{stage[1]}"))
                    elif kind == "get X2T":
                        b, n = misc(seg, i, stage)
                        act.wait_ge(misc_ready[b], n + 1)
                        A(x2T[:, :], m_ps[b][:, :], ACT.Identity, bias=vec("ln1_b"), scale=vec("ln1_w"))
                        A(x2bT[:, :], m_ps[b][:, :], ACT.Identity, bias=bln[:, 0:1],
                          scale=vec("ln1_w")).then_inc(misc_left[b], 1)
                    elif kind == "get H":
                        _, l, c = stage
                        evac(seg, i, stage, hT[l][:, c, :], ACT.Relu, bias=vec(f"b1_{l}_{c}"))
                    elif kind == "LN" and stage[2] == 1:
                        l = stage[1]
                        n = (i - 3) * 2 + l
                        act.wait_ge(mean_ready, n + 1)
                        A(lnv[:, l, :], mv[:, l, :, 1], ACT.Ln, bias=epsc[:, 0:1]).then_inc(lnv_done, 1)
                        act.wait_ge(lnv_done, n + 1)
                        A(rstd[:, l, :], lnv[:, l, :], ACT.Exp, scale=-0.5).then_inc(rstd_ready, 1)

            run(act, body)

        @block.vector
        def _(dve):
            v = nc.vector
            dve.wait_ge(const_loaded, 64)
            v.scalar_tensor_tensor(gtmp[:, 1, :], gtmp[:, 0, :], -1.0, gtmp[:, 0, :], ALU.mult,
                                   ALU.max).then_inc(setup_dve, 1)
            for f, name in enumerate(("bq0", "bq1", "bk2")):
                v.tensor_scalar(bqs[:, f:f + 1], vec(name), SCALE, None, ALU.mult).then_inc(setup_dve, 1)
            v.memset(epsc[:, 0:1], EPS)
            v.memset(epsc[:, 1:2], TINY).then_inc(setup_dve, 1)
            v.tensor_tensor(bln[:, :], vec("ln1_b"), vec("b2_1"), ALU.add).then_inc(setup_dve, 1)
            dve.wait_ge(setup_act, 2)
            v.tensor_scalar(gtmp[:, 0, :], gtmp[:, 0, :], 0.0, None, ALU.max).then_inc(setup_dve, 1)
            dve.wait_ge(setup_dve, 7)
            v.tensor_tensor(gtmp[:, 1, :], gtmp[:, 0, :], gtmp[:, 3, :], ALU.add).then_inc(setup_dve, 1)
            dve.wait_ge(setup_dve, 8)
            v.tensor_tensor(gamma2[:, :], gtmp[:, 1, :], gtmp[:, 1, :], ALU.mult).then_inc(setup_dve, 1)
            dve.wait_ge(setup_dve, 9)

            def heads(ap):
                return ap.rearrange("p (h k) -> p h k", k=SEQ)

            def body(seg, i):
                for stage in SEGMENTS[seg]:
                    kind = stage[0]
                    if kind == "get":
                        stage = stage[1:]
                        kind = "get " + stage[0]
                    if kind == "MASK":
                        f = stage[1]
                        dve.wait_ge(mask_loaded[f], 16 * (i - f + 1))
                        v.tensor_scalar(bias[f][:, :, :], min_[f][:, :, :], 1.0, -NEG0, ALU.subtract,
                                        ALU.mult).then_inc(bias_done[f], 1)
                        v.tensor_reduce(out=some[f][:, :], in_=min_[f][:, :, :], op=ALU.max,
                                        axis=AX.X).then_inc(bias_done[f], 1)
                    elif kind == "KM" and stage[1] not in KM_ON_ACT:
                        f = stage[1]
                        if f < 2:
                            dve.wait_ge(*left(seg, i, ("K", f)))
                        else:
                            dve.wait_ge(misc_left[0], all_left(seg, i, 0))
                            dve.wait_ge(misc_left[1], all_left(seg, i, 1))
                        for h in range(HH):
                            last = v.tensor_scalar(km[f][:, h, :], kT[f][:, :], head_rows[:, h:h + 1], None,
                                                   ALU.mult)
                        last.then_inc(km_ready[f], 1)
                    elif kind == "D1":
                        _, f, p = stage
                        l = layer(f)
                        u, slot = score_turn(seg, i, f, p)
                        n = PAIR_SCORES.number(seg, i, ("S", f, p))
                        c, _, _ = PAIR_SCORES.at(seg, i, ("S", f, p))
                        if l == 0 and p == 0:
                            dve.wait_ge(bias_done[f], 2 * (i - f + 1))
                        dve.wait_ge(sub_done[l], count(2 * (u - 1)))
                        for g in range(2):
                            bank = s_ps[(2 * c + g) % 3]
                            dve.wait_ge(scores_ready, 2 * n + g + 1)
                            if l == 0:
                                v.scalar_tensor_tensor(heads(sm[0][:, slot, g, :]), heads(bank[:, :]),
                                                       some[f][:, p:p + 1],
                                                       bias[f][:, None, p, :].broadcast_to([P, HH, SEQ]),
                                                       ALU.mult, ALU.add).then_inc(scores_left, 1)
                            else:
                                v.tensor_tensor(heads(sm[1][:, slot, g, :]), heads(bank[:, :]),
                                                causal[:, None, :].broadcast_to([P, HH, SEQ]),
                                                ALU.add).then_inc(scores_left, 1)
                        for g in range(2):
                            dve.wait_ge(scores_left, 2 * n + g + 1)
                            v.tensor_reduce(out=mx[l][:, slot, g, :], in_=heads(sm[l][:, slot, g, :]), op=ALU.max,
                                            axis=AX.X).then_inc(max_ready[l], 1)
                    elif kind == "D2":
                        p = stage[2]
                        u, slot = score_turn(seg, i, 2, p)
                        dve.wait_ge(exp1_done, u + 1)
                        dve.wait_ge(dist_done, u)
                        flat = slice(H * SEQ - 1, None, -1)
                        v.tensor_tensor_scan(suf[:, :, :].rearrange("p h k -> p (h k)")[:, flat], carry[:, flat],
                                             ex[:, :, :].rearrange("p h k -> p (h k)")[:, flat], 0.0,
                                             ALU.mult, ALU.add).then_inc(scan_done, 1)
                        dve.wait_ge(scan_done, u + 1)
                        dve.wait_ge(scaled_done, count(u - 1))
                        v.reciprocal(rtot[:, slot, :], suf[:, :, 0]).then_inc(rtot_done, 1)
                        dve.wait_ge(rtot_done, u + 1)
                        v.tensor_tensor(cc[:, slot, :], gamma2[:, :], rtot[:, slot, :],
                                        ALU.mult).then_inc(cc_ready, 1)
                    elif kind == "D3":
                        p = stage[2]
                        u, slot = score_turn(seg, i, 2, p)
                        t = te[:, slot, :, :].rearrange("p h k -> p (h k)")
                        dve.wait_ge(effect_ready, u + 1)
                        v.scalar_tensor_tensor(t, t, 1.0e-5, sm[1][:, slot, :, :].rearrange("p g c -> p (g c)"),
                                               ALU.max, ALU.mult).then_inc(s2_done, 1)
                        dve.wait_ge(s2_done, u + 1)
                        dve.wait_ge(sub2_done, count(u - 1))
                        v.tensor_reduce(out=mx2[:, slot, :, :].rearrange("p g h -> p (g h)"), in_=te[:, slot, :, :],
                                        op=ALU.max, axis=AX.X).then_inc(max2_ready, 1)
                    elif kind == "N":
                        _, f, p = stage
                        t = PAIR_TAILS.number(seg, i, ("T", f, p))
                        slot = PAIR_TAILS.slot(seg, i, ("T", f, p), 2)
                        o = o_ps[:, 0:HH * VW].rearrange("p (h g c) -> p g h c", h=HH, g=2)
                        z = rz[:, slot, :].rearrange("p (g h) -> p g h", g=2)
                        dve.wait_ge(pv_done, t + 1)
                        v.reciprocal(z, o[:, :, :, DK]).then_inc(rz_done, 1)
                        dve.wait_ge(rz_done, t + 1)
                        v.tensor_tensor(on[f][:, p, :].rearrange("p (g h d) -> p g h d", g=2, h=HH),
                                        o[:, :, :, 0:DK], z[:, :, :, None].broadcast_to([P, 2, HH, DK]),
                                        ALU.mult).then_inc(norm_done, 1)
                    elif kind == "get OP":
                        f = stage[1]
                        b, n = misc(seg, i, stage)
                        dve.wait_ge(misc_ready[b], n + 1)
                        if f == 0 and seg >= 2:
                            dve.wait_ge(*left(seg, i, ("OP", 1)))
                        v.scalar_tensor_tensor((xB, xF)[f][:, :], m_ps[b][:, :], vec(f"bo{f}"), (xA, xB)[f][:, :],
                                               ALU.add, ALU.add).then_inc(misc_left[b], 1)
                    elif kind == "get Y0":
                        b, n = misc(seg, i, stage)
                        dve.wait_ge(misc_ready[b], n + 1)
                        dve.wait_ge(xlb_done, count(i - 2))
                        v.scalar_tensor_tensor(xL[:, :], m_ps[b][:, :], vec("b2_0"), xF[:, :],
                                               ALU.add, ALU.add).then_inc(misc_left[b], 1)
                    elif kind == "LN" and stage[2] == 0:
                        l = stage[1]
                        n = (i - 3) * 2 + l
                        b, k = misc(seg, i, ("Y1",) if l else ("OP", 2))
                        dve.wait_ge(misc_ready[b], k + 1)
                        for j in range(PAIRS):
                            v.bn_stats(st6[:, l, j, :], m_ps[b][:, j * P:(j + 1) * P]).then_inc(stats_done, 1)
                        for j in range(PAIRS):
                            dve.wait_ge(stats_done, n * PAIRS + j + 1)
                            dve.nop(nofuse=True)
                            dve.nop(nofuse=True)
                            last = v.bn_aggr(mv[:, l, j, :], st6[:, l, j, :])
                        last.then_inc(mean_ready, 1)
                    elif kind == "NX":
                        l = stage[1]
                        n = (i - 3) * 2 + l
                        b, _ = misc(seg, i, ("Y1",) if l else ("OP", 2))
                        dve.wait_ge(rstd_ready, n + 1)
                        if l:
                            dve.wait_ge(y_ready, i - 2)
                        for j in range(PAIRS):
                            last = v.tensor_scalar(xn[:, l, j, :], m_ps[b][:, j * P:(j + 1) * P], mv[:, l, j, 0:1],
                                                   rstd[:, l, j:j + 1], ALU.subtract, ALU.mult)
                        last.then_inc(misc_left[b], 1)

            run(dve, body)

        @block.gpsimd
        def _(pool):
            g_ = nc.gpsimd
            pool.wait_ge(const_loaded, 64)
            for f in range(3):
                for n in range(2 * PAIRS):
                    last = g_.tensor_copy(vb[f][:, n, :, :].rearrange("p h c -> p (h c)"), vone)
                last.then_inc(setup_pool, 1)
            g_.memset(wd[:, :, SEQ - 1:SEQ], 0.0).then_inc(y_ready, 1)

            def body(seg, i):
                for stage in SEGMENTS[seg]:
                    kind = stage[0]
                    if kind == "SUB":
                        _, f, p = stage
                        l = layer(f)
                        u, slot = score_turn(seg, i, f, p)
                        if l == 0:
                            t = PAIR_TAILS.number(seg, i, ("T", f, p))
                            pool.wait_ge(shifted_t, count(2 * t - 2))
                        else:
                            pool.wait_ge(scan_done, u)
                        for g in range(2):
                            pool.wait_ge(max_ready[l], 2 * u + g + 1)
                            dst = ss[:, PAIR_TAILS.slot(seg, i, ("T", f, p), 2), :, g, :] if l == 0 else \
                                ex[:, HH * g:HH * g + HH, :]
                            g_.tensor_tensor(dst, sm[l][:, slot, g, :].rearrange("p (h k) -> p h k", k=SEQ),
                                             mx[l][:, slot, g, :, None].broadcast_to([P, HH, SEQ]),
                                             ALU.subtract).then_inc(sub_done[l], 1)
                    elif kind == "PM":
                        p = stage[2]
                        u, slot = score_turn(seg, i, 2, p)
                        pool.wait_ge(scan_done, u + 1)
                        pool.wait_ge(ln_done, u)
                        g_.tensor_tensor(wd[:, :, 0:SEQ - 1], suf[:, :, 1:SEQ],
                                         distance[:, None, 0:SEQ - 1].broadcast_to([P, H, SEQ - 1]),
                                         ALU.mult).then_inc(dist_done, 1)
                        pool.wait_ge(dist_done, u + 1)
                        pool.wait_ge(cc_ready, u + 1)
                        g_.tensor_tensor(wd[:, :, 0:SEQ - 1], wd[:, :, 0:SEQ - 1],
                                         cc[:, slot, :, None].broadcast_to([P, H, SEQ - 1]),
                                         ALU.mult).then_inc(scaled_done, 1)
                    elif kind == "SUB2":
                        p = stage[2]
                        u, slot = score_turn(seg, i, 2, p)
                        t = PAIR_TAILS.number(seg, i, ("T", 2, p))
                        pool.wait_ge(shifted_t, count(2 * t - 2))
                        pool.wait_ge(max2_ready, u + 1)
                        g_.tensor_tensor(ss[:, PAIR_TAILS.slot(seg, i, ("T", 2, p), 2), :, :, :]
                                         .rearrange("p h g k -> p g h k"),
                                         te[:, slot, :, :].rearrange("p (g h) k -> p g h k", g=2),
                                         mx2[:, slot, :, :, None].broadcast_to([P, 2, HH, SEQ]),
                                         ALU.subtract).then_inc(sub2_done, 1)
                    elif kind == "XLB":
                        pool.wait_ge(*left(seg, i, ("Y0",)))
                        if seg >= LOOP:
                            b, n = misc(seg, i, ("OP", 2))
                            pool.wait_ge(misc_ready[b], n + 1)
                        g_.tensor_tensor(xLb[:, :], xL[:, :], vec("bo2").broadcast_to([P, TOK]),
                                         ALU.add).then_inc(xlb_done, 1)
                    elif kind == "OUT":
                        pool.wait_ge(stored, 16 * (i - 2))
                        b, n = misc(seg, i, ("Y1",))
                        pool.wait_ge(misc_left[b], n + 1)
                        g_.tensor_tensor(yo[:, :, :], xn[:, 1, :, :],
                                         ln2[:, 0:1, :].broadcast_to([P, PAIRS, D]), ALU.mult).then_inc(gain_done, 1)
                        pool.wait_ge(gain_done, i - 2)
                        g_.tensor_tensor(yo[:, :, :], yo[:, :, :],
                                         ln2[:, 1:2, :].broadcast_to([P, PAIRS, D]), ALU.add).then_inc(y_ready, 1)

            run(pool, body)


def kernel(**inputs):
    import numpy as np
    import concourse.bacc as bacc
    from concourse.bass_utils import run_bass_kernel_spmd

    a = {n: np.asarray(v) for n, v in inputs.items()}
    f32 = np.float32

    def blocks(m):
        return m.reshape(CHUNKS, P, D).transpose(1, 0, 2).reshape(P, CHUNKS * D)

    l0, l1 = "L0_xattn_", "L1_xattn_"
    mats = {"q0": a[l0 + "sWq"], "k0": a[l0 + "sWk"], "v0": a[l0 + "sWv"], "o0": a[l0 + "sWo"],
            "q1": a[l0 + "cWq"], "k1": a[l0 + "cWk"], "v1": a[l0 + "cWv"], "o1": a[l0 + "cWo"],
            "w1_0": a[l0 + "W1"], "w2_0": blocks(a[l0 + "W2"]),
            "q2": a[l1 + "Wk"].T, "v2": a[l1 + "Wv"].T, "o2": a[l1 + "Wo"].T,
            "w1_1": a[l1 + "W1"].T, "w2_1": blocks(a[l1 + "W2"].T)}
    weights = np.concatenate([mats[n] for n in W_COLS], axis=1)
    small = {"bq0": "sbq", "bk0": "sbk", "bv0": "sbv", "bo0": "sbo", "bq1": "cbq", "bk1": "cbk", "bv1": "cbv",
             "bo1": "cbo", "b2_0": "b2"}
    small = {n: a[l0 + m] for n, m in small.items()}
    small.update({"bk2": a[l1 + "bk"], "bv2": a[l1 + "bv"], "bo2": a[l1 + "bo"], "ln1_w": a[l1 + "ln1_w"],
                  "ln1_b": a[l1 + "ln1_b"], "b2_1": a[l1 + "b2"]})
    for c in range(CHUNKS):
        small[f"b1_0_{c}"] = a[l0 + "b1"][c * P:(c + 1) * P]
        small[f"b1_1_{c}"] = a[l1 + "b1"][c * P:(c + 1) * P]
    vecs = np.stack([small[n] for n in VECS], axis=1)
    rows = np.broadcast_to(np.stack([a[l1 + "ln2_w"], a[l1 + "ln2_b"]]), (P, 2, D))
    gam = np.broadcast_to(a[l1 + "gammas"].reshape(1, H), (P, H))

    consts = np.zeros((P, C_TOTAL), f32)
    part = np.arange(P)
    consts[:, C_IDENT:C_IDENT + P] = np.eye(P)
    consts[:, C_HEAD:C_HEAD + HH] = (part[:, None] // DK) % HH == np.arange(HH)
    ahead = (part % SEQ)[:, None] - np.arange(SEQ)[None, :]
    consts[:, C_CAUSAL:C_CAUSAL + SEQ] = np.where(ahead >= 0, 0.0, NEG1)
    consts[:, C_DIST:C_DIST + SEQ] = np.maximum(ahead, 0)
    consts[:, C_CARRY:C_CARRY + H * SEQ] = np.tile(np.arange(SEQ) < SEQ - 1, H)
    ones = np.zeros((P, HH, VW), f32)
    ones[:P // 2, :, DK] = 1
    ones[P // 2:, :, 2 * DK + 1] = 1
    consts[:, C_VONE:] = ones.reshape(P, HH * VW)

    arrays = {"x": a["x"].reshape(-1, D), "ctx_in": a["ctx_1024"].reshape(-1, D),
              "mask0": a["mask_Bx1xSxS2_bk0"].reshape(-1, SEQ),
              "mask1": a["mask_Bx1xSxS2_bf1"].reshape(-1, SEQ),
              "weights": weights, "vecs": vecs, "rows": rows, "gam": gam, "consts": consts}
    arrays = {n: np.ascontiguousarray(v) for n, v in arrays.items()}
    nc = bacc.Bacc("TRN2", target_bir_lowering=False, num_devices=1)
    args = [nc.dram_tensor(n, v.shape, mybir.dt.from_np(v.dtype), kind="ExternalInput").ap()
            for n, v in arrays.items()]
    args.append(nc.dram_tensor("out", (NB * SEQ, D), mybir.dt.float32, kind="ExternalOutput").ap())
    build(nc, *args)
    r = run_bass_kernel_spmd(nc, [arrays], core_ids=[0])
    return r.results[0]["out"].reshape(NB, SEQ, D)
```
